# Optimizing a Trainium2 kernel written in Bass

```python
import numpy as np
import jax
import jax.numpy as jnp

def _softmax(x, axis=-1):
    return jax.nn.softmax(x, axis=axis)

def _gelu(x):
    return jax.nn.gelu(x, approximate=True)

def _silu(x):
    return jax.nn.silu(x)

def _sigmoid(x):
    return jax.nn.sigmoid(x)

def _layernorm(x, axis=-1, eps=1e-05):
    m = jnp.mean(x, axis=axis, keepdims=True)
    v = jnp.var(x, axis=axis, keepdims=True)
    return (x - m) / jnp.sqrt(v + eps)

def _scatter_add(tgt, idx, src, axis=0):
    return tgt.at[idx].add(src)

def _segment_sum(src, seg, n):
    return jax.ops.segment_sum(src, seg, n)
kernel_name = 'mk_xattn_seq_d1_seqx_r2_f32fa6'

def setup_inputs(seed: int=0):
    np.random.seed(seed)
    _w = jnp.asarray

    def _rec_inputs():
        import jax
        import jax.numpy as jnp
        _rk = jax.random.key(seed)
        x = -0.0001548 + 1 * jax.random.normal(jax.random.fold_in(_rk, 1), (2, 2048, 640), jnp.float32)
        _lenS = 2048 - jax.random.randint(jax.random.fold_in(_rk, 7), (2,), 0, max(1, 2048 // 4) + 1, jnp.int32)
        _lenS2 = 128 - jax.random.randint(jax.random.fold_in(_rk, 8), (2,), 0, max(1, 128 // 4) + 1, jnp.int32)
        _ctx_768P = jax.random.normal(jax.random.fold_in(_rk, 11), (2, 16, 384), jnp.float32)
        _ctx_768c = jax.random.dirichlet(jax.random.fold_in(_rk, 511), 0.3 * jnp.ones((16,), jnp.float32), (2, 128))
        _ctx_768t = jnp.einsum('bsk,bkd->bsd', _ctx_768c, _ctx_768P)
        _ctx_768t = _ctx_768t * jax.lax.rsqrt(jnp.mean(jnp.square(_ctx_768t)) + 1e-12) * 0.953939
        ctx_768 = 0.00141353 + 0.998943 * (_ctx_768t + 0.3 * jax.random.normal(jax.random.fold_in(_rk, 611), (2, 128, 384), jnp.float32))
        return (x, ctx_768)
    x, ctx_768 = _rec_inputs()

    def _L0_xattn_setup():
        import jax, jax.numpy as jnp
        import numpy as np
        HEADS = 8
        NUM_TOKENS = 4
        CROSS_ATTENTION_DIM = 384

        def _mha(q, k, v, heads=HEADS):
            B, Sq, H = q.shape
            Sk = k.shape[1]
            d = H // heads
            qh = q.reshape(B, Sq, heads, d).transpose(0, 2, 1, 3)
            kh = k.reshape(B, Sk, heads, d).transpose(0, 2, 1, 3)
            vh = v.reshape(B, Sk, heads, d).transpose(0, 2, 1, 3)
            scores = jnp.einsum('bhqd,bhkd->bhqk', qh, kh) * jnp.asarray(d, q.dtype) ** (-0.5)
            probs = jax.nn.softmax(scores, axis=-1)
            out = jnp.einsum('bhqk,bhkd->bhqd', probs, vh)
            return out.transpose(0, 2, 1, 3).reshape(B, Sq, H)
        key = jax.random.key(seed)
        ks = jax.random.split(key, 10)
        B, S, H, CAD, T = (4, 512, 640, CROSS_ATTENTION_DIM, NUM_TOKENS)
        sc = 0.02
        return {'hidden_states': jax.random.normal(ks[0], (B, S, H), jnp.float32), 'encoder_hidden_states': jax.random.normal(ks[1], (B, 77 + T, CAD), jnp.float32), 'Wq': jax.random.normal(ks[2], (H, H), jnp.float32) * sc, 'Wk': jax.random.normal(ks[3], (CAD, H), jnp.float32) * sc, 'Wv': jax.random.normal(ks[4], (CAD, H), jnp.float32) * sc, 'Wq_ca': jax.random.normal(ks[5], (T, H), jnp.float32) * sc, 'Wk_ca': jax.random.normal(ks[6], (CAD, H), jnp.float32) * sc, 'Wv_ca': jax.random.normal(ks[7], (CAD, H), jnp.float32) * sc, 'Wout': jax.random.normal(ks[8], (H, H), jnp.float32) * sc, 'b_out': jnp.zeros((H,), jnp.float32)}
    _L0_xattn_all = _L0_xattn_setup()
    _L0_xattn_in = {k: v for k, v in _L0_xattn_all.items() if k in ('Wq', 'Wk', 'Wv', 'Wq_ca', 'Wk_ca', 'Wv_ca', 'Wout', 'b_out')}
    del _L0_xattn_all
    return {'x': x, 'ctx_768': ctx_768, 'L0_xattn_Wq': _L0_xattn_in['Wq'], 'L0_xattn_Wk': _L0_xattn_in['Wk'], 'L0_xattn_Wv': _L0_xattn_in['Wv'], 'L0_xattn_Wq_ca': _L0_xattn_in['Wq_ca'], 'L0_xattn_Wk_ca': _L0_xattn_in['Wk_ca'], 'L0_xattn_Wv_ca': _L0_xattn_in['Wv_ca'], 'L0_xattn_Wout': _L0_xattn_in['Wout'], 'L0_xattn_b_out': _L0_xattn_in['b_out']}

def reference(x, ctx_768, L0_xattn_Wq, L0_xattn_Wk, L0_xattn_Wv, L0_xattn_Wq_ca, L0_xattn_Wk_ca, L0_xattn_Wv_ca, L0_xattn_Wout, L0_xattn_b_out):
    import jax
    import jax.numpy as jnp

    def _L0_xattn_ref(hidden_states, encoder_hidden_states, Wq, Wk, Wv, Wq_ca, Wk_ca, Wv_ca, Wout, b_out):
        import jax, jax.numpy as jnp
        import numpy as np
        HEADS = 8
        NUM_TOKENS = 4
        CROSS_ATTENTION_DIM = 384

        def _mha(q, k, v, heads=HEADS):
            B, Sq, H = q.shape
            Sk = k.shape[1]
            d = H // heads
            qh = q.reshape(B, Sq, heads, d).transpose(0, 2, 1, 3)
            kh = k.reshape(B, Sk, heads, d).transpose(0, 2, 1, 3)
            vh = v.reshape(B, Sk, heads, d).transpose(0, 2, 1, 3)
            scores = jnp.einsum('bhqd,bhkd->bhqk', qh, kh) * jnp.asarray(d, q.dtype) ** (-0.5)
            probs = jax.nn.softmax(scores, axis=-1)
            out = jnp.einsum('bhqk,bhkd->bhqd', probs, vh)
            return out.transpose(0, 2, 1, 3).reshape(B, Sq, H)
        residual = hidden_states
        unet_size = residual.shape[1]
        end_pos = encoder_hidden_states.shape[1] - NUM_TOKENS
        enc = encoder_hidden_states[:, :end_pos, :]
        ca = encoder_hidden_states[:, end_pos:, :]
        query = hidden_states @ Wq
        keyt = enc @ Wk
        valt = enc @ Wv
        hs = _mha(query, keyt, valt)
        ca_q1 = jnp.einsum('btc,th->bch', ca, Wq_ca)
        indices = np.linspace(0, CROSS_ATTENTION_DIM - 1, unet_size).astype(np.int64)
        ca_q1 = ca_q1[:, indices, :]
        ca_hs1 = _mha(ca_q1, residual, residual)
        ca_q2 = ca_hs1 @ Wq
        ca_k2 = ca @ Wk_ca
        ca_v2 = ca @ Wv_ca
        ca_hs2 = _mha(ca_q2, ca_k2, ca_v2)
        out = hs + ca_hs2
        out = out @ Wout + b_out
        out = out + residual
        return out
    x = _L0_xattn_ref(x, ctx_768, L0_xattn_Wq, L0_xattn_Wk, L0_xattn_Wv, L0_xattn_Wq_ca, L0_xattn_Wk_ca, L0_xattn_Wv_ca, L0_xattn_Wout, L0_xattn_b_out)
    return x

_drawn_inputs = setup_inputs


def setup_inputs(seed=0):
    import zlib

    import numpy as np

    out = dict(_drawn_inputs(seed))
    spreads = {'L0_xattn_b_out': (0.0, 0.1)}
    factors = {'L0_xattn_Wq': 7.813, 'L0_xattn_Wk': 7.767, 'L0_xattn_Wq_ca': 8.0, 'L0_xattn_Wk_ca': 8.0}
    for name, (base, spread) in spreads.items():
        noise = np.random.default_rng([zlib.crc32(name.encode()), seed]).standard_normal(out[name].shape)
        drawn = base * np.exp(spread * noise) if base else spread * noise
        out[name] = jnp.asarray(drawn.astype(out[name].dtype))
    for name, factor in factors.items():
        out[name] = (out[name] * factor).astype(out[name].dtype)
    return out
```

```python
import numpy as np
import concourse.bass as bass
from concourse import mybir
from contextlib import ExitStack

F32, F32R = mybir.dt.float32, mybir.dt.float32r
ALU, ACT, AX = mybir.AluOpType, mybir.ActivationFunctionType, mybir.AxisListType

P = 128
B, S, H = 2, 2048, 640
NH, D = 8, 80
CAD = 384
NT = 4
NK = P - NT
SCALE = float(D) ** -0.5
TILES = S // P
KT = H // P
CT = CAD // P
SETS, R = 2, 4
SW = R * NK
BANK = 512
SLOTS = 32
HALF = H // 2


def gather_pairs():
    index = np.linspace(0, CAD - 1, S).astype(np.int64)
    assert (index == (np.arange(S) * (CAD - 1)) // (S - 1)).all()
    return [(i, c) for i in range(TILES)
            for c in range(index[i * P] // P, index[i * P + P - 1] // P + 1)]


def build(nc, x, ctx_in, wq, wk, wv, wqca, wkca, wvca, wout, bout, out):
    pairs = gather_pairs()
    ctx = ExitStack()
    with ctx:
        def sb(name, shape, dt=F32):
            return ctx.enter_context(nc.sbuf_tensor(name, shape, dt))

        def sem(name):
            return ctx.enter_context(nc.semaphore(name))

        ident = sb("ident", [P, P])
        headmask = sb("headmask", [P, KT, NH])
        wca = sb("wca", [P, KT, NH, NT])
        sel = sb("sel", [P, len(pairs), P])
        kv = sb("kv", [D + 1, NH, 2, P])
        wh = sb("wh", [D + 1, NH, H])
        mm_hi = sb("mm_hi", [P, KT * SETS * BANK], F32R)
        mm_lo = sb("mm_lo", [P, KT * SETS * BANK], F32R)
        wk2 = sb("wk2", [P, KT, NH, NT])
        xin = sb("xin", [P, 2, H])
        xb = sb("xb", [P, 4, R, D + 1])
        negmax = sb("negmax", [P, 2, NH])
        top = sb("top", [P, 2, NH])
        sums = sb("sums", [P, 2, NH])
        rinv = sb("rinv", [P, TILES, NH])
        gs = sb("gs", [P, 2, NH, SLOTS])
        as_ = sb("as_", [P, CT, NH, SLOTS])
        aT = sb("aT", [P, SETS, CAD], F32R)
        gk = sb("gk", [P, 4, P], F32R)
        mraw = sb("mraw", [P, CT, NH])
        rl = sb("rl", [P, CT, NH])
        s2 = sb("s2", [P, CT * NH, NT])
        e2 = sb("e2", [P, CT * NH, NT])
        m2 = sb("m2", [P, CT * NH])
        l2 = sb("l2", [P, CT * NH])
        r2 = sb("r2", [P, CT * NH])
        p2 = sb("p2", [P, CT, NH * NT])
        p2x = sb("p2x", [P, TILES, NH, NT])

        with nc.sbuf_tensor("ex", [P, TILES, NH, NK], F32) as ex:
            pass
        with (nc.sbuf_tensor("wq_in", [P, KT, H], F32) as wq_in, nc.sbuf_tensor("wkv_in", [P, 4, CT, H], F32) as wkv_in,
              nc.sbuf_tensor("ctx_tok", [P, CAD], F32) as ctx_tok, nc.sbuf_tensor("ctxT", [P, CT, P], F32) as ctxT,
              nc.sbuf_tensor("ones_row", [1, P], F32) as ones_row, nc.sbuf_tensor("wqca_in", [NT, H], F32) as wqca_in):
            pass
        reserve_ex = sb("reserve_ex", [P, TILES * NH * NK])
        with nc.sbuf_tensor("hs1", [P, CT, NH, D], F32) as hs1:
            pass
        with nc.sbuf_tensor("e", [P, R, CAD], F32) as e:
            pass
        xT_hi = sb("xT_hi", [P, 2, KT, P], F32R)
        xT_lo = sb("xT_lo", [P, 2, KT, P], F32R)
        with nc.sbuf_tensor("gT", [P, SETS, S], F32R) as gT:
            pass
        with nc.sbuf_tensor("hs1T", [P, CT, KT, P], F32) as hs1T:
            pass
        probs = sb("probs", [P, 2, NH, P])
        pT_hi = sb("pT_hi", [P, 2, NH, P], F32R)
        pT_lo = sb("pT_lo", [P, 2, NH, P], F32R)
        res = sb("res", [P, 2, H])

        PS = ctx.enter_context(nc.psum_tensor("PS", [P, 8, BANK], F32))

        def flat(first, banks=2):
            return PS[:, first:first + banks, :].rearrange("p b n -> p (b n)")

        def scores_of(u):
            return PS[:, 4 + 2 * u:6 + 2 * u, :]

        def g_of(u):
            return scores_of(u)[:, :, SW:SW + R * NT].rearrange("p s (r t) -> p s r t", r=R)

        def mm(half):
            return half[:, :].rearrange("p (k s n) -> p k s n", k=KT, s=SETS)

        def vw(half):
            return half[:, :].rearrange("p (h f n) -> p h f n", h=NH, f=2)

        def nsum_of(h):
            return wh[:, :, :].rearrange("p h n -> p (h n)")[:, h * CAD:(h + 1) * CAD]

        sel_made, mask_made, gs_set = sem("sel_made"), sem("mask_made"), sem("gs_set")
        ident0, ident_made = sem("ident0"), sem("ident_made")
        wca_ps, wca_made = sem("wca_ps"), sem("wca_made")
        ctx_in_s, wkv_in_s, wq_in_s, wout_in_s = sem("ctx_loaded"), sem("wkv_loaded"), sem("wq_loaded"), sem("wout_loaded")
        ctxT_ps, ctxT_made, as_hi, as_made = sem("ctxT_ps"), sem("ctxT_made"), sem("as_hi"), sem("as_made")
        wqT_ps, wqT_made = sem("wqT_ps"), sem("wqT_made")
        kv_ps, kv_made = sem("kv_ps"), sem("kv_made")
        mm_ps, mmh_made, mml_made = sem("mm_ps"), sem("mmh_made"), sem("mml_made")
        x_in = [sem("x_in0"), sem("x_in1")]
        xT_ps, xTh_made, xTl_made = sem("xT_ps"), sem("xTh_made"), sem("xTl_made")
        sc_ps, top_made, negmax_made, exp_made = sem("sc_ps"), sem("top_made"), sem("negmax_made"), sem("exp_made")
        gs_hi, gs_made, gT_ps, gT_made = sem("gs_hi"), sem("gs_made"), sem("gT_ps"), sem("gT_made")
        rinv_made = sem("rinv_made")
        vw_ps, vwh_made, vwl_made = sem("vw_ps"), sem("vwh_made"), sem("vwl_made")
        aT_ps, aT_made = sem("aT_ps"), sem("aT_made")
        mx_ps, mx_made, asm_hi, asm_made = sem("mx_ps"), sem("mx_made"), sem("asm_hi"), sem("asm_made")
        xb_in = [sem(f"xb_in{k}") for k in range(4)]
        gk_made, sT_ps, e_made, pv_done, ns_made = sem("gk_made"), sem("sT_ps"), sem("e_made"), sem("pv_done"), sem("ns_made")
        nT_ps, rl_made, hs1_made, hT_ps, hT_made = sem("nT_ps"), sem("rl_made"), sem("hs1_made"), sem("hT_ps"), sem("hT_made")
        s2_ps, m2_made, s2_made, e2_made = sem("s2_ps"), sem("m2_made"), sem("s2_made"), sem("e2_made")
        l2_made, r2_made, p2_made, p2x_ps, p2x_made = sem("l2_made"), sem("r2_made"), sem("p2_made"), sem("p2x_ps"), sem("p2x_made")
        probs_made, pT_ps, pTh_made, pTl_made = sem("probs_made"), sem("pT_ps"), sem("pTh_made"), sem("pTl_made")
        out_ps, res_made = sem("out_ps"), sem("res_made")
        stored = [sem("stored0"), sem("stored1")]

        block = ctx.enter_context(nc.Block())
        x_rows = x.rearrange("b s n -> (b s) n")
        out_rows = out.rearrange("b s n -> (b s) n")

        @block.sync
        def _(sp):
            sp.dma_start(wqca_in[:, :], wqca).then_inc(stored[0], 16)
            sp.wait_ge(mask_made, 3)
            sp.dma_start(kv[D:D + 1, 0, 1, :], ones_row[:, :]).then_inc(stored[1], 16)
            with sp.Fori(0, B) as b:
                sp.wait_ge(probs_made, 1 + b * TILES)
                sp.dma_start(ctx_tok[:, :], ctx_in.rearrange("b t n -> (b t) n")[bass.ds(b * P, P), :]).then_inc(ctx_in_s, 16)
                for n, w in enumerate((wk, wkca, wv, wvca)):
                    sp.dma_start(wkv_in[:, n], w.rearrange("(c p) n -> p c n", p=P)).then_inc(wkv_in_s, 16)
                sp.dma_start(wq_in[:, :, :], wq.rearrange("(j p) n -> p j n", p=P)).then_inc(wq_in_s, 16)

                def load_x(i, u):
                    sp.dma_start(xin[:, u, :], x_rows[bass.ds(b * S + i * P, P), :]).then_inc(x_in[u], 16)

                sp.wait_ge(res_made, 1 + b * TILES)
                load_x(0, 0)
                load_x(1, 1)
                with sp.Fori(1, TILES // 2) as ni:
                    i = ni * 2
                    for u in range(2):
                        sp.wait_ge(xT_ps, b * TILES + i + (u - 1))
                        load_x(i + u, u)
                sp.wait_ge(mm_ps, (b + 1) * KT * SETS)
                sp.dma_start(wh[0:D, :, :], wout.rearrange("(h d) n -> d h n", d=D)).then_inc(wout_in_s, 16)
                sp.dma_start(wh[D:D + 1, 0, :], bout.rearrange("(a n) -> a n", a=1)).then_inc(wout_in_s, 16)
                for s in range(SETS):
                    def load_xb(kt, k):
                        sp.dma_start(xb[:, k, :, 0:D],
                                     x_rows[bass.ds(b * S + kt * P, P), s * R * D:(s + 1) * R * D]
                                     .rearrange("p (r d) -> p r d", r=R)).then_inc(xb_in[k], 16)
                    for k in range(4):
                        if s:
                            sp.wait_ge(pv_done, b * 128 + 52 + 4 * k)
                        load_xb(k, k)
                    with sp.Fori(1, TILES // 4) as nkt:
                        kt = nkt * 4
                        for k in range(4):
                            sp.wait_ge(pv_done, b * 128 + s * 64 + kt * 4 + (4 * k - 12))
                            load_xb(kt + k, k)
                sp.wait_ge(xT_ps, (b + 1) * TILES)
                load_x(0, 0)
                load_x(1, 1)

                def store(i, u):
                    sp.wait_ge(res_made, 1 + b * TILES + i + 1)
                    sp.dma_start(out_rows[bass.ds(b * S + i * P, P), :], res[:, u, :]).then_inc(stored[u], 16)
                with sp.Fori(0, TILES // 2 - 1) as ni:
                    i = ni * 2
                    for u in range(2):
                        store(i + u, u)
                        load_x(i + (u + 2), u)
                for u in range(2):
                    store(TILES - 2 + u, u)
            for u in range(2):
                sp.wait_ge(stored[u], 16 + B * TILES // 2 * 16)

        @block.gpsimd
        def _(pool):
            nc.gpsimd.memset(ident[:, :], 0.0).then_inc(ident0, 1)
            nc.gpsimd.memset(probs[:, :, :, :], 0.0).then_inc(probs_made, 1)
            nc.gpsimd.memset(headmask[:, :, :], 1.0).then_inc(ident0, 1)
            pool.wait_ge(ident0, 2)
            nc.gpsimd.affine_select(out=ident[:, :], in_=ident[:, :], compare_op=ALU.not_equal, fill=1.0, base=0,
                                    pattern=[[-1, P]], channel_multiplier=1).then_inc(ident_made, 1)
            nc.gpsimd.affine_select(out=headmask[:, :, :], in_=headmask[:, :, :], compare_op=ALU.is_ge, fill=0.0, base=0,
                                    pattern=[[P, KT], [-D, NH]], channel_multiplier=1).then_inc(ident0, 1)
            pool.wait_ge(ident0, 3)
            nc.gpsimd.affine_select(out=headmask[:, :, :], in_=headmask[:, :, :], compare_op=ALU.is_gt, fill=0.0, base=D,
                                    pattern=[[-P, KT], [D, NH]], channel_multiplier=-1).then_inc(mask_made, 1)
            nc.gpsimd.memset(ones_row[:, :], 1.0).then_inc(mask_made, 1)
            pool.wait_ge(mask_made, 2)
            nc.gpsimd.memset(ones_row[:, NK:P], 0.0).then_inc(mask_made, 1)
            nc.gpsimd.memset(sel[:, :, :], 1.0).then_inc(sel_made, 1)
            pool.wait_ge(sel_made, 1)
            for n, (i, c) in enumerate(pairs):
                base = (CAD - 1) * P * i - (S - 1) * P * c
                nc.gpsimd.affine_select(out=sel[:, n, :], in_=sel[:, n, :], compare_op=ALU.is_ge, fill=0.0, base=base,
                                        pattern=[[CAD - 1, P]], channel_multiplier=-(S - 1)).then_inc(sel_made, 1)
            pool.wait_ge(sel_made, 1 + len(pairs))
            for n, (i, c) in enumerate(pairs):
                base = (CAD - 1) * P * i - (S - 1) * P * c
                nc.gpsimd.affine_select(out=sel[:, n, :], in_=sel[:, n, :], compare_op=ALU.is_gt, fill=0.0,
                                        base=(S - 1) - base, pattern=[[-(CAD - 1), P]],
                                        channel_multiplier=S - 1).then_inc(sel_made, 1)
            with pool.Fori(0, B) as b:
                pool.wait_ge(p2x_made, b + 1)
                def normalise(i, u):
                    nc.gpsimd.tensor_tensor(probs[:, u, :, 0:NK], ex[:, bass.ds(i, 1)].rearrange("p a h k -> p (a h) k"),
                                            rinv[:, bass.ds(i, 1), :].rearrange("p a h -> p (a h)").unsqueeze(2)
                                            .broadcast_to([P, NH, NK]), ALU.mult)
                    nc.gpsimd.tensor_copy(probs[:, u, :, NK:P], p2x[:, bass.ds(i, 1)].rearrange("p a h k -> p (a h) k"))\
                        .then_inc(probs_made, 1)
                normalise(0, 0)
                normalise(1, 1)
                with pool.Fori(1, TILES // 2) as ni:
                    i = ni * 2
                    for u in range(2):
                        pool.wait_ge(pT_ps, b * TILES + i + (u - 1))
                        normalise(i + u, u)

        @block.scalar
        def _(act):
            with act.Fori(0, B) as b:
                for h in range(NH):
                    act.wait_ge(wqT_ps, b * NH + h + 1)
                    nc.scalar.activation(wh[0:D, h, :], flat(2 * (h % 2))[0:D, 0:H], ACT.Copy).then_inc(wqT_made, 1)
                for n in range(KT * SETS):
                    act.wait_ge(mm_ps, b * KT * SETS + n + 1)
                    nc.scalar.activation(mm(mm_hi)[:, n // 2, n % 2, 0:SW].rearrange("p (r k) -> p r k", r=R),
                                         PS[:, n % 4, :].rearrange("p (r k) -> p r k", r=R)[:, :, 0:NK],
                                         ACT.Copy).then_inc(mmh_made, 1)

                def xT(i, u, ring=True):
                    act.wait_ge(xT_ps, b * TILES + i + 1)
                    if ring:
                        act.wait_ge(sc_ps, b * TILES + i + (-1))
                    nc.scalar.activation(xT_hi[:, u].rearrange("p k n -> p (k n)"), flat(0)[:, 0:H],
                                         ACT.Copy).then_inc(xTh_made, 1)

                def soft(i, u):
                    act.wait_ge(negmax_made, b * TILES + i + 1)
                    for h in range(NH):
                        last = nc.scalar.activation(
                            ex[:, bass.ds(i, 1), h, :].rearrange("p a k -> p (a k)"),
                            scores_of(u)[:, h // R, (h % R) * NK:(h % R + 1) * NK], ACT.Exp,
                            bias=negmax[:, u, h:h + 1], scale=SCALE, accum_out=sums[:, u, h:h + 1])
                    last.then_inc(exp_made, 1)

                def g(i):
                    act.wait_ge(gT_ps, b * TILES + i + 1)
                    nc.scalar.activation(gT[:, :, bass.ds(i * P, P)], PS[:, 2, 0:SETS * P].rearrange("p (s n) -> p s n", s=SETS),
                                         ACT.Copy).then_inc(gT_made, 1)

                xT(0, 0, False)
                xT(1, 1, False)
                soft(0, 0)
                with act.Fori(0, TILES // 2 - 1) as ni:
                    i = ni * 2 + 1
                    for v in range(2):
                        xT(i + (v + 1), v)
                        soft(i + v, 1 - v)
                        g(i + (v - 1))
                soft(TILES - 1, 1)
                g(TILES - 2)
                g(TILES - 1)
                for n in range(2 * NH):
                    act.wait_ge(vw_ps, b * 2 * NH + n + 1)
                    nc.scalar.activation(vw(mm_hi)[:, n // 2, n % 2, :], PS[:, n % 4, 0:HALF], ACT.Copy).then_inc(vwh_made, 1)
                act.wait_ge(aT_ps, b * 3 + 1)
                nc.scalar.activation(aT[:, 0, :], PS[:, 4, 0:CAD], ACT.Copy).then_inc(aT_made, 1)
                for s in range(SETS):
                    act.wait_ge(aT_ps, b * 3 + 2 + s)
                    nc.scalar.activation(aT[:, s, :], PS[:, s, 0:CAD], ACT.Copy).then_inc(aT_made, 1)
                for s in range(SETS):
                    def key_exps(kt, first=False):
                        for r in range(R):
                            act.wait_ge(sT_ps, b * 128 + s * 64 + kt * 4 + (r + 1))
                            if not first:
                                act.wait_ge(pv_done, b * 128 + s * 64 + kt * 4 + (r - 3))
                            nc.scalar.activation(e[:, r, :], PS[:, 4 + r, 0:CAD], ACT.Exp, scale=SCALE).then_inc(e_made, 1)
                    key_exps(0, s == 0)
                    with act.Fori(1, TILES) as kt:
                        key_exps(kt)
                for c in range(CT):
                    act.wait_ge(hT_ps, b * CT + c + 1)
                    nc.scalar.activation(hs1T[:, c].rearrange("p k n -> p (k n)"), flat((6, 0, 2)[c])[:, 0:H],
                                         ACT.Copy).then_inc(hT_made, 1)
                act.wait_ge(s2_made, b + 1)
                nc.scalar.activation(e2[:, :, :], s2[:, :, :], ACT.Exp, scale=SCALE).then_inc(e2_made, 1)

                def pT(i, u, ring=True):
                    act.wait_ge(pT_ps, b * TILES + i + 1)
                    if ring:
                        act.wait_ge(out_ps, b * TILES + i + (-1))
                    nc.scalar.activation(pT_hi[:, u].rearrange("p h n -> p (h n)"), flat(2 * u), ACT.Copy).then_inc(pTh_made, 1)
                pT(0, 0, False)
                pT(1, 1, False)
                with act.Fori(1, TILES // 2) as ni:
                    i = ni * 2
                    for u in range(2):
                        pT(i + u, u)

        @block.vector
        def _(dve):
            nc.vector.memset(gs[:, :, :, :], 0.0).then_inc(gs_set, 1)
            nc.vector.memset(as_[:, :, :, :], 0.0).then_inc(gs_set, 1)
            nc.vector.memset(xb[:, :, :, :], 1.0).then_inc(gs_set, 1)
            nc.vector.memset(res[:, :, :], 0.0).then_inc(res_made, 1)
            dve.wait_ge(gs_set, 1)
            nc.vector.memset(gs[:, :, :, 16:18], 1.0).then_inc(gs_set, 1)
            dve.wait_ge(wca_ps, 1)
            dve.wait_ge(mask_made, 3)
            for j in range(KT):
                last = nc.vector.tensor_tensor(wca[:, j], PS[:, 0, j * NT:(j + 1) * NT].unsqueeze(1).broadcast_to([P, NH, NT]),
                                               headmask[:, j, :].unsqueeze(2).broadcast_to([P, NH, NT]), ALU.mult)
            last.then_inc(wca_made, 1)
            with dve.Fori(0, B) as b:
                dve.wait_ge(ctxT_ps, b + 1)
                nc.vector.tensor_copy(ctxT[:, :, :].rearrange("p c n -> p (c n)"), PS[:, 0, 0:CAD]).then_inc(ctxT_made, 1)
                dve.wait_ge(ctxT_made, b + 1)
                dve.wait_ge(gs_set, 4)

                def as_half(c, lo):
                    return as_[:, c, :, 0:16].rearrange("p h (a l t) -> p h a l t", a=2, l=2)[:, :, :, lo, :]

                def ca(c):
                    return ctxT[:, c, NK:P].unsqueeze(1).unsqueeze(1).broadcast_to([P, NH, 2, NT])
                for c in range(CT):
                    nc.vector.tensor_copy(as_half(c, 0).bitcast(F32R), ca(c)).then_inc(as_hi, 1)
                dve.wait_ge(as_hi, (b + 1) * CT)
                for c in range(CT):
                    nc.vector.tensor_tensor(as_half(c, 1).bitcast(F32R), ca(c), as_half(c, 0), ALU.subtract).then_inc(as_made, 1)
                for n in range(4):
                    dve.wait_ge(kv_ps, b * 4 + n + 1)
                    nc.vector.tensor_copy(kv[0:D, 2 * n:2 * n + 2].rearrange("p h a n -> p (h a n)"),
                                          PS[0:D, 4 + n, :]).then_inc(kv_made, 1)
                dve.wait_ge(wca_made, 1)
                for n in range(KT * SETS):
                    j, s = n // 2, n % 2
                    ps = PS[:, n % 4, :].rearrange("p (r k) -> p r k", r=R)
                    dve.wait_ge(mmh_made, b * KT * SETS + n + 1)
                    nc.vector.tensor_tensor(mm(mm_lo)[:, j, s, 0:SW].rearrange("p (r k) -> p r k", r=R), ps[:, :, 0:NK],
                                            mm(mm_hi)[:, j, s, 0:SW].bitcast(F32).rearrange("p (r k) -> p r k", r=R), ALU.subtract)
                    nc.vector.tensor_copy(wk2[:, j, s * R:(s + 1) * R, :], ps[:, :, NK:P]).then_inc(mml_made, 1)
                for s in range(SETS):
                    nc.vector.tensor_copy(mm(mm_hi)[:, :, s, SW:BANK], wca[:, :, s * R:(s + 1) * R, :].rearrange("p k r t -> p k (r t)"))\
                        .then_inc(mml_made, 1)
                dve.wait_ge(mml_made, b * 14 + 12)
                for s in range(SETS):
                    nc.vector.tensor_tensor(mm(mm_lo)[:, :, s, SW:BANK], wca[:, :, s * R:(s + 1) * R, :].rearrange("p k r t -> p k (r t)"),
                                            mm(mm_hi)[:, :, s, SW:BANK].bitcast(F32), ALU.subtract).then_inc(mml_made, 1)

                def xT(i, u):
                    dve.wait_ge(xTh_made, b * TILES + i + 1)
                    nc.vector.tensor_tensor(xT_lo[:, u].rearrange("p k n -> p (k n)"), flat(0)[:, 0:H],
                                            xT_hi[:, u].bitcast(F32).rearrange("p k n -> p (k n)"), ALU.subtract).then_inc(xTl_made, 1)

                def gs_half(u, s, lo):
                    return gs[:, u, s * R:(s + 1) * R, 8 * lo:8 * lo + 8].rearrange("p r (a t) -> p r a t", a=2)

                def g_rep(u, s):
                    return g_of(u)[:, s].unsqueeze(2).broadcast_to([P, R, 2, NT])

                def soft(i, u, first=False):
                    dve.wait_ge(sc_ps, b * TILES + i + 1)
                    if not first:
                        dve.wait_ge(exp_made, b * TILES + i + (-1))
                    nc.vector.tensor_reduce(top[:, u, :].rearrange("p (s r) -> p s r", s=SETS), scores_of(u)[:, :, 0:SW].rearrange("p s (r k) -> p s r k", r=R),
                                            AX.X, ALU.max).then_inc(top_made, 1)
                    if not first:
                        dve.wait_ge(gT_ps, b * TILES + i + (-1))
                    for s in range(SETS):
                        nc.vector.tensor_copy(gs_half(u, s, 0).bitcast(F32R), g_rep(u, s)).then_inc(gs_hi, 1)
                    dve.wait_ge(gs_hi, b * 2 * TILES + i * 2 + 2)
                    for s in range(SETS):
                        last = nc.vector.tensor_tensor(gs_half(u, s, 1).bitcast(F32R), g_rep(u, s), gs_half(u, s, 0), ALU.subtract)
                    last.then_inc(gs_made, 1)
                    dve.wait_ge(top_made, b * TILES + i + 1)
                    dve.wait_ge(gs_made, b * TILES + i + 1)
                    nc.vector.tensor_scalar(negmax[:, u, :], top[:, u, :], -SCALE, None, ALU.mult).then_inc(negmax_made, 1)

                def inv(i, u):
                    dve.wait_ge(exp_made, b * TILES + i + 1)
                    nc.vector.reciprocal(rinv[:, bass.ds(i, 1), :].rearrange("p a h -> p (a h)"), sums[:, u, :]).then_inc(rinv_made, 1)

                xT(0, 0)
                xT(1, 1)
                soft(0, 0, True)
                inv(0, 0)
                xT(2, 0)
                soft(1, 1, True)
                with dve.Fori(1, TILES // 2 - 1) as ni:
                    i = ni * 2
                    for u in range(2):
                        xT(i + (u + 1), 1 - u)
                        inv(i + (u - 1), 1 - u)
                        soft(i + u, u)
                xT(TILES - 1, 1)
                inv(TILES - 3, 1)
                soft(TILES - 2, 0)
                inv(TILES - 2, 0)
                soft(TILES - 1, 1)
                inv(TILES - 1, 1)
                for n in range(2 * NH):
                    dve.wait_ge(vwh_made, b * 2 * NH + n + 1)
                    nc.vector.tensor_tensor(vw(mm_lo)[:, n // 2, n % 2, :], PS[:, n % 4, 0:HALF],
                                            vw(mm_hi)[:, n // 2, n % 2, :].bitcast(F32), ALU.subtract).then_inc(vwl_made, 1)
                for n in range(CT * NH):
                    c, h = n // NH, n % NH
                    dve.wait_ge(mx_ps, b * CT * NH + n + 1)
                    nc.vector.tensor_reduce(mraw[:, c, h:h + 1], flat(4 * (n % 2), 4), AX.X, ALU.max).then_inc(mx_made, 1)
                dve.wait_ge(mx_made, (b + 1) * CT * NH)
                nc.vector.tensor_scalar(as_[:, :, :, 16].bitcast(F32R), mraw[:, :, :], -1.0, None, ALU.mult).then_inc(asm_hi, 1)
                dve.wait_ge(asm_hi, b + 1)
                nc.vector.scalar_tensor_tensor(as_[:, :, :, 17].bitcast(F32R), mraw[:, :, :], -1.0, as_[:, :, :, 16],
                                               ALU.mult, ALU.subtract).then_inc(asm_made, 1)
                for s in range(SETS):
                    def key_stack(kt, k):
                        nc.vector.tensor_copy(gk[:, k, :], gT[:, s, bass.ds(kt * P, P)].bitcast(F32)).then_inc(gk_made, 1)
                    for k in range(4):
                        if s:
                            dve.wait_ge(sT_ps, b * 128 + 52 + 4 * k)
                        else:
                            dve.wait_ge(gT_made, (b + 1) * TILES)
                        key_stack(k, k)
                    with dve.Fori(1, TILES // 4) as nkt:
                        kt = nkt * 4
                        for k in range(4):
                            dve.wait_ge(sT_ps, b * 128 + s * 64 + kt * 4 + (4 * k - 12))
                            key_stack(kt + k, k)
                    dve.wait_ge(pv_done, b * 128 + (s + 1) * 64)
                    for r in range(R):
                        h = s * R + r
                        nc.vector.tensor_copy(nsum_of(h), PS[0:D + 1, r, 0:CAD]).then_inc(ns_made, 1)
                for c in range(CT):
                    ps = PS[:, 2 * c:2 * c + 2, 0:R * (D + 1)].rearrange("p s (r d) -> p s r d", r=R)
                    dve.wait_ge(nT_ps, b * CT + c + 1)
                    nc.vector.reciprocal(rl[:, c, :].rearrange("p (s r) -> p s r", s=SETS), ps[:, :, :, D]).then_inc(rl_made, 1)
                    dve.wait_ge(rl_made, b * CT + c + 1)
                    for s in range(SETS):
                        last = nc.vector.tensor_tensor(hs1[:, c, s * R:(s + 1) * R, :], ps[:, s, :, 0:D],
                                                       rl[:, c, s * R:(s + 1) * R].unsqueeze(2).broadcast_to([P, R, D]), ALU.mult)
                    last.then_inc(hs1_made, 1)
                dve.wait_ge(s2_ps, b + 1)
                sc2 = PS[:, 4, 0:CT * NH * NT].rearrange("p (g t) -> p g t", t=NT)
                nc.vector.tensor_reduce(m2[:, :], sc2, AX.X, ALU.max).then_inc(m2_made, 1)
                dve.wait_ge(m2_made, b + 1)
                nc.vector.tensor_tensor(s2[:, :, :], sc2, m2[:, :].unsqueeze(2).broadcast_to([P, CT * NH, NT]), ALU.subtract).then_inc(s2_made, 1)
                dve.wait_ge(e2_made, b + 1)
                nc.vector.tensor_reduce(l2[:, :], e2[:, :, :], AX.X, ALU.add).then_inc(l2_made, 1)
                dve.wait_ge(l2_made, b + 1)
                nc.vector.reciprocal(r2[:, :], l2[:, :]).then_inc(r2_made, 1)
                dve.wait_ge(r2_made, b + 1)
                nc.vector.tensor_tensor(p2[:, :, :].rearrange("p c (h t) -> p (c h) t", t=NT), e2[:, :, :],
                                        r2[:, :].unsqueeze(2).broadcast_to([P, CT * NH, NT]), ALU.mult).then_inc(p2_made, 1)
                dve.wait_ge(p2x_ps, b + 1)
                nc.vector.tensor_copy(p2x[:, :, :, :].rearrange("p i h t -> p (i h t)"), PS[:, 5, :]).then_inc(p2x_made, 1)

                def pT(i, u):
                    dve.wait_ge(pTh_made, b * TILES + i + 1)
                    nc.vector.tensor_tensor(pT_lo[:, u].rearrange("p h n -> p (h n)"), flat(2 * u),
                                            pT_hi[:, u].bitcast(F32).rearrange("p h n -> p (h n)"), ALU.subtract).then_inc(pTl_made, 1)

                def add_x(i, u):
                    dve.wait_ge(out_ps, b * TILES + i + 1)
                    dve.wait_ge(x_in[u], b * TILES * 16 + (TILES // 2 + 1) * 16 + (i - u) * 8)
                    dve.wait_ge(stored[u], 16 + b * (TILES // 2) * 16 + (i - u) * 8)
                    nc.vector.tensor_tensor(res[:, u, :].rearrange("p (f n) -> p f n", f=2), PS[:, 4 + 2 * u:6 + 2 * u, 0:HALF],
                                            xin[:, u, :].rearrange("p (f n) -> p f n", f=2), ALU.add).then_inc(res_made, 1)
                pT(0, 0)
                with dve.Fori(0, TILES // 2 - 1) as ni:
                    i = ni * 2
                    for u in range(2):
                        pT(i + (u + 1), 1 - u)
                        add_x(i + u, u)
                pT(TILES - 1, 1)
                add_x(TILES - 2, 0)
                add_x(TILES - 1, 1)

        @block.tensor
        def _(pe):
            mul = nc.tensor.matmul
            for u in range(2):
                pe.wait_ge(stored[u], 16)
            pe.wait_ge(ident_made, 1)
            for j in range(KT):
                last = nc.tensor.transpose(PS[:, 0, j * NT:(j + 1) * NT], wqca_in[:, j * P:(j + 1) * P], ident[0:NT, 0:NT])
            last.then_inc(wca_ps, 1)
            pe.wait_ge(mask_made, 3)
            with pe.Fori(0, B) as b:
                pe.wait_ge(wca_made, 1)
                pe.wait_ge(ctx_in_s, b * 16 + 16)
                for c in range(CT):
                    last = nc.tensor.transpose(PS[:, 0, c * P:(c + 1) * P], ctx_tok[:, c * P:(c + 1) * P], ident[:, :])
                last.then_inc(ctxT_ps, 1)
                pe.wait_ge(res_made, 1 + b * TILES)
                pe.wait_ge(ctxT_made, b + 1)
                pe.wait_ge(wkv_in_s, (b + 1) * 64)
                for h in range(NH):
                    for a in range(2):
                        at = (h % 2) * 256 + a * P
                        for w, t0, t1 in ((2 * a, 0, NK), (2 * a + 1, NK, P)):
                            for c in range(CT):
                                last = mul(PS[0:D, 4 + h // 2, at + t0:at + t1], wkv_in[:, w, c, h * D:(h + 1) * D],
                                           ctxT[:, c, t0:t1], start=(c == 0), stop=(c == CT - 1))
                    if h % 2:
                        last.then_inc(kv_ps, 1)
                pe.wait_ge(wq_in_s, (b + 1) * 16)
                for h in range(NH):
                    if h >= 2:
                        pe.wait_ge(wqT_made, b * NH + h - 1)
                    for j in range(KT):
                        last = nc.tensor.transpose(flat(2 * (h % 2))[0:D, j * P:(j + 1) * P], wq_in[:, j, h * D:(h + 1) * D], ident[:, :])
                    last.then_inc(wqT_ps, 1)
                pe.wait_ge(kv_made, (b + 1) * 4)
                pe.wait_ge(wqT_made, (b + 1) * NH)
                for n in range(KT * SETS):
                    if n >= 4:
                        pe.wait_ge(mml_made, b * 14 + n - 3)
                    for r in range(R):
                        h = (n % 2) * R + r
                        last = mul(PS[:, n % 4, r * P:(r + 1) * P], wh[0:D, h, (n // 2) * P:(n // 2 + 1) * P], kv[0:D, h, 0, :],
                                   start=True, stop=True)
                    last.then_inc(mm_ps, 1)

                def xT(i, u, first=False):
                    pe.wait_ge(x_in[u], b * TILES * 16 + (i - u) * 8 + 16)
                    if not first:
                        pe.wait_ge(xTl_made, b * TILES + i)
                    for j in range(KT):
                        last = nc.tensor.transpose(flat(0)[:, j * P:(j + 1) * P], xin[:, u, j * P:(j + 1) * P], ident[:, :])
                    last.then_inc(xT_ps, 1)

                def scores(i, u, first=False):
                    pe.wait_ge(xTl_made, b * TILES + i + 1)
                    if not first:
                        pe.wait_ge(exp_made, b * TILES + i + (-1))
                        pe.wait_ge(gs_made, b * TILES + i + (-1))
                    for j in range(KT):
                        for n, (l, rr) in enumerate(((xT_hi, mm_hi), (xT_hi, mm_lo), (xT_lo, mm_hi))):
                            for s in range(SETS):
                                last = mul(scores_of(u)[:, s, :], l[:, u, j, :], mm(rr)[:, j, s, :],
                                           start=(j == 0 and n == 0), stop=(j == KT - 1 and n == 2))
                    last.then_inc(sc_ps, 1)

                def g(i, u, first=False):
                    pe.wait_ge(gs_made, b * TILES + i + 1)
                    if not first:
                        pe.wait_ge(gT_made, b * TILES + i)
                    for s in range(SETS):
                        last = nc.tensor.transpose(PS[:, 2, s * P:(s + 1) * P],
                                                   gs[:, u, s * R:(s + 1) * R, :].rearrange("p r n -> p (r n)"), ident[:, :])
                    last.then_inc(gT_ps, 1)

                pe.wait_ge(mml_made, (b + 1) * 14)
                xT(0, 0, True)
                xT(1, 1)
                scores(0, 0, True)
                xT(2, 0)
                scores(1, 1, True)
                g(0, 0, True)
                with pe.Fori(1, TILES // 2 - 1) as ni:
                    i = ni * 2
                    for u in range(2):
                        xT(i + (u + 1), 1 - u)
                        scores(i + u, u)
                        g(i + (u - 1), 1 - u)
                xT(TILES - 1, 1)
                scores(TILES - 2, 0)
                g(TILES - 3, 1)
                scores(TILES - 1, 1)
                g(TILES - 2, 0)
                g(TILES - 1, 1)

                pe.wait_ge(wout_in_s, (b + 1) * 32)
                pe.wait_ge(gT_made, (b + 1) * TILES)
                for n in range(2 * NH):
                    h, f = n // 2, n % 2
                    if n >= 4:
                        pe.wait_ge(vwl_made, b * 2 * NH + n - 3)
                    rows = D + 1 if h == 0 else D
                    mul(PS[:, n % 4, 0:HALF], kv[0:rows, h, 1, :], wh[0:rows, h, f * HALF:(f + 1) * HALF],
                        start=True, stop=True).then_inc(vw_ps, 1)

                pe.wait_ge(as_made, (b + 1) * CT)
                pe.wait_ge(exp_made, (b + 1) * TILES)
                pe.wait_ge(gs_made, (b + 1) * TILES)
                for c in range(CT):
                    last = nc.tensor.transpose(PS[:, 4, c * P:(c + 1) * P], as_[:, c, 0:R, :].rearrange("p r n -> p (r n)"), ident[:, :])
                last.then_inc(aT_ps, 1)
                pe.wait_ge(aT_made, b * 3 + 1)
                pe.wait_ge(vwl_made, (b + 1) * 2 * NH)
                for n in range(CT * NH):
                    c, h = n // NH, n % NH
                    r = h % R
                    if n >= 2:
                        pe.wait_ge(mx_made, b * CT * NH + n - 1)
                    for q in range(4):
                        last = mul(PS[:, 4 * (n % 2) + q, :], aT[r * SLOTS:r * SLOTS + 16, 0, c * P:(c + 1) * P],
                                   gT[r * SLOTS:r * SLOTS + 16, h // R, q * BANK:(q + 1) * BANK], start=True, stop=True)
                    last.then_inc(mx_ps, 1)
                pe.wait_ge(asm_made, b + 1)
                for s in range(SETS):
                    for c in range(CT):
                        last = nc.tensor.transpose(PS[:, s, c * P:(c + 1) * P],
                                                   as_[:, c, s * R:(s + 1) * R, :].rearrange("p r n -> p (r n)"), ident[:, :])
                    last.then_inc(aT_ps, 1)
                pe.wait_ge(aT_made, b * 3 + 3)
                for s in range(SETS):
                    base = s * 64

                    def sT(kt, k, r):
                        if r == 0:
                            pe.wait_ge(gk_made, b * 2 * TILES + s * TILES + kt + 1)
                        mul(PS[:, 4 + r, 0:CAD], gk[r * SLOTS:r * SLOTS + 18, k, :], aT[r * SLOTS:r * SLOTS + 18, s, :],
                            start=True, stop=True).then_inc(sT_ps, 1)

                    def pv(kt, k, r, start, stop, n):
                        pe.wait_ge(e_made, b * 128 + base + kt * 4 + (r + 1))
                        if r == 0:
                            pe.wait_ge(xb_in[k], b * 128 + s * 64 + (kt - k) * 4 + 16)
                        mul(PS[0:D + 1, r, 0:CAD], xb[:, k, r, :], e[:, r, :], start=start, stop=stop).then_inc(pv_done, 1)

                    for r in range(R):
                        sT(0, 0, r)
                    if s:
                        pe.wait_ge(ns_made, b * NH + R)
                    for kt in range(4):
                        for r in range(R):
                            pv(kt, kt, r, kt == 0, False, 0)
                            sT(kt + 1, (kt + 1) % 4, r)
                    with pe.Fori(1, TILES // 4 - 1) as nkt:
                        kt = nkt * 4
                        for k in range(4):
                            for r in range(R):
                                pv(kt + k, k, r, False, False, 0)
                                sT(kt + (k + 1), (k + 1) % 4, r)
                    for k in range(4):
                        for r in range(R):
                            pv(TILES - 4 + k, k, r, False, k == 3, 0)
                            if k < 3:
                                sT(TILES - 3 + k, k + 1, r)
                pe.wait_ge(ns_made, (b + 1) * NH)
                for c in range(CT):
                    for h in range(NH):
                        at = (h % R) * (D + 1)
                        last = nc.tensor.transpose(PS[:, 2 * c + h // R, at:at + D + 1], nsum_of(h)[:, c * P:(c + 1) * P],
                                                   ident[0:D + 1, 0:D + 1])
                    last.then_inc(nT_ps, 1)
                for c in range(CT):
                    pe.wait_ge(hs1_made, b * CT + c + 1)
                    for j in range(KT):
                        last = nc.tensor.transpose(flat((6, 0, 2)[c])[:, j * P:(j + 1) * P],
                                                   hs1[:, c].rearrange("p h d -> p (h d)")[:, j * P:(j + 1) * P], ident[:, :])
                    last.then_inc(hT_ps, 1)
                for c in range(CT):
                    pe.wait_ge(hT_made, b * CT + c + 1)
                    for j in range(KT):
                        last = mul(PS[:, 4, c * 32:(c + 1) * 32], hs1T[:, c, j, :], wk2[:, j].rearrange("p h t -> p (h t)"),
                                   start=(j == 0), stop=(j == KT - 1))
                last.then_inc(s2_ps, 1)
                pe.wait_ge(sel_made, 1 + 2 * len(pairs))
                pe.wait_ge(p2_made, b + 1)
                for n, (i, c) in enumerate(pairs):
                    last = mul(PS[:, 5, i * 32:(i + 1) * 32], sel[:, n, :], p2[:, c, :],
                               start=(n == 0 or pairs[n - 1][0] != i), stop=(n + 1 == len(pairs) or pairs[n + 1][0] != i))
                last.then_inc(p2x_ps, 1)

                def pT(i, u, first=False):
                    pe.wait_ge(probs_made, 1 + b * TILES + i + 1)
                    if not first:
                        pe.wait_ge(pTl_made, b * TILES + i + (-1))
                    for h in range(NH):
                        last = nc.tensor.transpose(flat(2 * u)[:, h * P:(h + 1) * P], probs[:, u, h, :], ident[:, :])
                    last.then_inc(pT_ps, 1)

                def output(i, u, first=False):
                    pe.wait_ge(pTl_made, b * TILES + i + 1)
                    if not first:
                        pe.wait_ge(res_made, 1 + b * TILES + i + (-1))
                    for h in range(NH):
                        for n, (l, rr) in enumerate(((pT_hi, mm_hi), (pT_hi, mm_lo), (pT_lo, mm_hi))):
                            for f in range(2):
                                last = mul(PS[:, 4 + 2 * u + f, 0:HALF], l[:, u, h, :], vw(rr)[:, h, f, :],
                                           start=(h == 0 and n == 0), stop=(h == NH - 1 and n == 2))
                    last.then_inc(out_ps, 1)

                pT(0, 0, True)
                pe.wait_ge(p2x_made, b + 1)
                pT(1, 1, True)
                output(0, 0, True)
                pT(2, 0)
                output(1, 1, True)
                with pe.Fori(1, TILES // 2 - 1) as ni:
                    i = ni * 2
                    for u in range(2):
                        pT(i + (u + 1), 1 - u)
                        output(i + u, u)
                pT(TILES - 1, 1)
                output(TILES - 2, 0)
                output(TILES - 1, 1)


_INS = ['x', 'ctx_768', 'L0_xattn_Wq', 'L0_xattn_Wk', 'L0_xattn_Wv', 'L0_xattn_Wq_ca', 'L0_xattn_Wk_ca', 'L0_xattn_Wv_ca',
        'L0_xattn_Wout', 'L0_xattn_b_out']


def kernel(**inputs):
    import concourse.bacc as bacc
    from concourse.bass_utils import run_bass_kernel_spmd as run

    nc = bacc.Bacc("TRN2", target_bir_lowering=False, num_devices=1)
    arrays, args = {}, []
    for name in _INS:
        a = np.ascontiguousarray(inputs[name])
        arrays[f"in_{name}"] = a
        args.append(nc.dram_tensor(f"in_{name}", a.shape, mybir.dt.from_np(a.dtype), kind="ExternalInput").ap())
    args.append(nc.dram_tensor("out_0", (B, S, H), F32, kind="ExternalOutput").ap())
    build(nc, *args)
    r = run(nc, [arrays], core_ids=[0])
    return r.results[0]["out_0"]
```

```python
import numpy as np
import concourse.bass as bass
from concourse import mybir
from contextlib import ExitStack

F32, F32R = mybir.dt.float32, mybir.dt.float32r
ALU, ACT, AX = mybir.AluOpType, mybir.ActivationFunctionType, mybir.AxisListType

P = 128
B, S, H = 2, 2048, 640
NH, D = 8, 80
CAD = 384
NT = 4
NK = P - NT
SCALE = float(D) ** -0.5
TILES = S // P
KT = H // P
CT = CAD // P
SETS, R = 2, 4
SW = R * NK
BANK = 512
SLOTS = 32
HALF = H // 2
CHUNKS = 6
UNITS = CT * NH // 2
MXB = (CHUNKS + 1) * UNITS


def gather_pairs():
    index = np.linspace(0, CAD - 1, S).astype(np.int64)
    assert (index == (np.arange(S) * (CAD - 1)) // (S - 1)).all()
    return [(i, c) for i in range(TILES)
            for c in range(index[i * P] // P, index[i * P + P - 1] // P + 1)]


def build(nc, x, ctx_in, wq, wk, wv, wqca, wkca, wvca, wout, bout, out):
    pairs = gather_pairs()
    ctx = ExitStack()
    with ctx:
        def sb(name, shape, dt=F32):
            return ctx.enter_context(nc.sbuf_tensor(name, shape, dt))

        def sem(name):
            return ctx.enter_context(nc.semaphore(name))

        ident = sb("ident", [P, P])
        one = sb("one", [P, 1])
        headmask = sb("headmask", [P, KT, NH])
        wca = sb("wca", [P, KT, NH, NT])
        sel = sb("sel", [P, len(pairs), P])
        kv = sb("kv", [D + 1, NH, 2, P])
        wh = sb("wh", [D + 1, NH, H])
        mm_hi = sb("mm_hi", [P, KT * SETS * BANK], F32R)
        mm_lo = sb("mm_lo", [P, KT * SETS * BANK], F32R)
        wk2 = sb("wk2", [P, KT, NH, NT])
        xin = sb("xin", [P, 2, H])
        xb = sb("xb", [P, 4, R, D + 1])
        negmax = sb("negmax", [P, 2, NH])
        top = sb("top", [P, 2, NH])
        sums = sb("sums", [P, 2, NH])
        rinv = sb("rinv", [P, TILES, NH])
        gs = sb("gs", [P, 2, NH, SLOTS])
        as_ = sb("as_", [P, CT, NH, SLOTS])
        aT = sb("aT", [P, SETS, CAD], F32R)
        gk = sb("gk", [P, 4, P], F32R)
        mpart = sb("mpart", [P, CHUNKS + 1, CT * NH])
        mraw = sb("mraw", [P, CT, NH])
        caT = sb("caT", [P, B, CT, NT])
        rl = sb("rl", [P, CT, NH])
        s2 = sb("s2", [P, CT * NH, NT])
        e2 = sb("e2", [P, CT * NH, NT])
        m2 = sb("m2", [P, CT * NH])
        l2 = sb("l2", [P, CT * NH])
        r2 = sb("r2", [P, CT * NH])
        p2 = sb("p2", [P, CT, NH * NT])
        p2x = sb("p2x", [P, TILES, NH, NT])

        with nc.sbuf_tensor("ex", [P, TILES, NH, NK], F32) as ex:
            pass
        with (nc.sbuf_tensor("wq_in", [P, KT, H], F32) as wq_in, nc.sbuf_tensor("wkv_in", [P, 4, CT, H], F32) as wkv_in,
              nc.sbuf_tensor("ctx_tok", [P, B, CAD], F32) as ctx_tok, nc.sbuf_tensor("ctxT", [P, CT, B, P], F32) as ctxT,
              nc.sbuf_tensor("ones_row", [1, P], F32) as ones_row, nc.sbuf_tensor("wqca_in", [NT, H], F32) as wqca_in):
            pass
        reserve_ex = sb("reserve_ex", [P, TILES * NH * NK])
        with nc.sbuf_tensor("hs1", [P, CT, NH, D], F32) as hs1:
            pass
        with nc.sbuf_tensor("e", [P, R, CAD], F32) as e:
            pass
        with nc.sbuf_tensor("kv_next", [D, NH, 2, P], F32) as kv_next:
            pass
        xT_hi = sb("xT_hi", [P, 2, KT, P], F32R)
        xT_lo = sb("xT_lo", [P, 2, KT, P], F32R)
        with nc.sbuf_tensor("gT", [P, SETS, S], F32R) as gT:
            with nc.sbuf_tensor("aTm", [P, R, CAD], F32R) as aTm:
                pass
            with nc.sbuf_tensor("ns0", [D + 1, R, CAD], F32) as ns0:
                pass
        with nc.sbuf_tensor("ns1", [D + 1, R, CAD], F32) as ns1:
            pass
        with nc.sbuf_tensor("hs1T", [P, CT, KT, P], F32) as hs1T:
            pass
        probs = sb("probs", [P, 2, NH, P])
        pT_hi = sb("pT_hi", [P, 2, NH, P], F32R)
        pT_lo = sb("pT_lo", [P, 2, NH, P], F32R)
        res = sb("res", [P, 2, H])

        PS = ctx.enter_context(nc.psum_tensor("PS", [P, 8, BANK], F32))

        def flat(first, banks=2):
            return PS[:, first:first + banks, :].rearrange("p b n -> p (b n)")

        def scores_of(u):
            return PS[:, 4 + 2 * u:6 + 2 * u, :]

        def g_of(u):
            return scores_of(u)[:, :, SW:SW + R * NT].rearrange("p s (r t) -> p s r t", r=R)

        def e_half(half):
            return half[:, 0:R * CAD].rearrange("p (r n) -> p r n", r=R)

        def xb_half(half):
            return half[:, R * CAD:R * CAD + 4 * R * (D + 1)].rearrange("p (k n) -> p k n", k=4)

        def mm(half):
            return half[:, :].rearrange("p (k s n) -> p k s n", k=KT, s=SETS)

        def vw(half):
            return half[:, :].rearrange("p (h f n) -> p h f n", h=NH, f=2)

        def nsum_of(h):
            return (ns0, ns1)[h // R][:, h % R, :]

        wqT_kept = nc.dram_tensor("wqT_kept", (D, NH, H), F32, kind="Internal").ap()
        kv_kept = nc.dram_tensor("kv_kept", (D, NH, 2, P), F32, kind="Internal").ap()

        sel_made, mask_made, gs_set = sem("sel_made"), sem("mask_made"), sem("gs_set")
        ident0, ident_made = sem("ident0"), sem("ident_made")
        wca_ps, wca_made = sem("wca_ps"), sem("wca_made")
        ctx_in_s, wkv_in_s, wq_in_s, wout_in_s = sem("ctx_loaded"), [sem("wk_loaded"), sem("wv_loaded")], sem("wq_loaded"), sem("wout_loaded")
        caT_made = sem("caT_made")
        ctxT_ps, ctxT_made, as_hi, as_made = sem("ctxT_ps"), sem("ctxT_made"), sem("as_hi"), sem("as_made")
        wqT_ps, wqT_made = sem("wqT_ps"), sem("wqT_made")
        kv_ps, kv_made = sem("kv_ps"), sem("kv_made")
        mm_ps, mmh_made, mml_made = sem("mm_ps"), sem("mmh_made"), sem("mml_made")
        x_in = [sem("x_in0"), sem("x_in1")]
        xT_ps, xTh_made, xTl_made = sem("xT_ps"), sem("xTh_made"), sem("xTl_made")
        sc_ps, top_made, negmax_made, exp_made = sem("sc_ps"), sem("top_made"), sem("negmax_made"), sem("exp_made")
        gs_hi, gs_made, gT_ps, gT_made = sem("gs_hi"), sem("gs_made"), sem("gT_ps"), sem("gT_made")
        rinv_made = sem("rinv_made")
        vw_ps, vwh_made, vwl_made = sem("vw_ps"), sem("vwh_made"), sem("vwl_made")
        aT_ps, aT_made = sem("aT_ps"), sem("aT_made")
        mx_ps, mx_made, asm_hi, asm_made = sem("mx_ps"), sem("mx_made"), sem("asm_hi"), sem("asm_made")
        xb_in = [sem(f"xb_in{k}") for k in range(4)]
        xh_made, xl_made, ehi_made, elo_made, elo3_made = (sem("xh_made"), sem("xl_made"), sem("ehi_made"), sem("elo_made"),
                                                           sem("elo3_made"))
        kept, reload_in, aTm_zero, aTm_ps, aTm_made = (sem("kept"), sem("reload_in"), sem("aTm_zero"), sem("aTm_ps"),
                                                       sem("aTm_made"))
        mpart_made = sem("mpart_made")
        nsa_made, nsd_made = sem("nsa_made"), sem("nsd_made")
        gk_made, sT_ps, e_made, pv_done, eh3_made = sem("gk_made"), sem("sT_ps"), sem("e_made"), sem("pv_done"), sem("eh3_made")
        nT_ps, rl_made, hs1_made, hT_ps, hT_made = sem("nT_ps"), sem("rl_made"), sem("hs1_made"), sem("hT_ps"), sem("hT_made")
        s2_ps, m2_made, s2_made, e2_made = sem("s2_ps"), sem("m2_made"), sem("s2_made"), sem("e2_made")
        l2_made, r2_made, p2_made, p2x_ps, p2x_made = sem("l2_made"), sem("r2_made"), sem("p2_made"), sem("p2x_ps"), sem("p2x_made")
        probs_made, pT_ps, pTh_made, pTl_made = sem("probs_made"), sem("pT_ps"), sem("pTh_made"), sem("pTl_made")
        out_ps, res_made = sem("out_ps"), sem("res_made")
        stored = [sem("stored0"), sem("stored1")]

        block = ctx.enter_context(nc.Block())
        x_rows = x.rearrange("b s n -> (b s) n")
        out_rows = out.rearrange("b s n -> (b s) n")

        @block.sync
        def _(sp):
            sp.dma_start(wqca_in[:, :], wqca).then_inc(stored[0], 16)
            sp.dma_start(wq_in[:, :, :], wq.rearrange("(j p) n -> p j n", p=P)).then_inc(wq_in_s, 16)
            sp.dma_start(ctx_tok[:, :, :], ctx_in.rearrange("b t n -> t b n")).then_inc(ctx_in_s, 16)
            for w, ready in ((wk, 0), (wkca, 1), (wv, 2), (wvca, 3)):
                sp.dma_start(wkv_in[:, ready], w.rearrange("(c p) n -> p c n", p=P)).then_inc(wkv_in_s[ready // 2], 16)
            sp.wait_ge(mask_made, 3)
            sp.dma_start(kv[D:D + 1, 0, 1, :], ones_row[:, :]).then_inc(stored[1], 16)
            sp.wait_ge(wqT_made, NH)
            sp.dma_start(wqT_kept, wh[0:D, :, :]).then_inc(kept, 16)
            sp.wait_ge(kv_made, 2 * NH)
            sp.dma_start(kv_kept, kv_next[:, :, :, :]).then_inc(kept, 16)
            sp.dma_start(wqca_in[:, :], wqca).then_inc(reload_in, 16)
            for b in range(B):
                def load_x(i, u):
                    sp.dma_start(xin[:, u, :], x_rows[bass.ds(i * P + b * S, P), :]).then_inc(x_in[u], 16)

                if b:
                    sp.wait_ge(res_made, 1 + b * TILES)
                load_x(0, 0)
                load_x(1, 1)
                with sp.Fori(1, TILES // 2) as ni:
                    i = ni * 2
                    for u in range(2):
                        sp.wait_ge(xT_ps, i + (b * TILES + u - 1))
                        load_x(i + u, u)
                sp.wait_ge(mm_ps, (b + 1) * KT * SETS)
                sp.wait_ge(kept, 32)
                sp.dma_start(wh[0:D, :, :], wout.rearrange("(h d) n -> d h n", d=D)).then_inc(wout_in_s, 16)
                sp.dma_start(wh[D:D + 1, 0, :], bout.rearrange("(a n) -> a n", a=1)).then_inc(wout_in_s, 16)
                for s in range(SETS):
                    def load_xb(kt, k):
                        sp.dma_start(xb[:, k, :, 0:D], x_rows[bass.ds(kt * P + b * S, P), s * R * D:(s + 1) * R * D]
                                     .rearrange("p (r d) -> p r d", r=R)).then_inc(xb_in[k], 16)
                    for k in range(4):
                        if b or s:
                            sp.wait_ge(xl_made, b * 2 * TILES + s * TILES + k - 3)
                        load_xb(k, k)
                    with sp.Fori(1, TILES // 4) as nkt:
                        kt = nkt * 4
                        for k in range(4):
                            sp.wait_ge(xl_made, kt + (b * 2 * TILES + s * TILES + k - 3))
                            load_xb(kt + k, k)
                sp.wait_ge(xT_ps, (b + 1) * TILES)
                load_x(0, 0)
                load_x(1, 1)
                if b + 1 < B:
                    sp.wait_ge(vw_ps, (b + 1) * 2 * NH)
                    sp.dma_start(wh[0:D, :, :], wqT_kept).then_inc(reload_in, 16)
                    sp.dma_start(kv[0:D], kv_kept).then_inc(reload_in, 16)

                def store(i, u):
                    sp.wait_ge(res_made, i + (b * TILES + 2))
                    sp.dma_start(out_rows[bass.ds(i * P + b * S, P), :], res[:, u, :]).then_inc(stored[u], 16)
                with sp.Fori(0, TILES // 2 - 1) as ni:
                    i = ni * 2
                    for u in range(2):
                        store(i + u, u)
                        load_x(i + (u + 2), u)
                for u in range(2):
                    store(TILES - 2 + u, u)
            for u in range(2):
                sp.wait_ge(stored[u], 16 + B * TILES // 2 * 16)
            sp.wait_ge(kept, 32)

        @block.gpsimd
        def _(pool):
            nc.gpsimd.memset(one[:, :], 1.0).then_inc(ident0, 1)
            nc.gpsimd.memset(ident[:, :], 0.0).then_inc(ident0, 1)
            nc.gpsimd.memset(headmask[:, :, :], 1.0).then_inc(ident0, 1)
            pool.wait_ge(ident0, 3)
            nc.gpsimd.affine_select(out=ident[:, :], in_=ident[:, :], compare_op=ALU.not_equal, fill=1.0, base=0,
                                    pattern=[[-1, P]], channel_multiplier=1).then_inc(ident_made, 1)
            nc.gpsimd.affine_select(out=headmask[:, :, :], in_=headmask[:, :, :], compare_op=ALU.is_ge, fill=0.0, base=0,
                                    pattern=[[P, KT], [-D, NH]], channel_multiplier=1).then_inc(ident0, 1)
            pool.wait_ge(ident0, 4)
            nc.gpsimd.affine_select(out=headmask[:, :, :], in_=headmask[:, :, :], compare_op=ALU.is_gt, fill=0.0, base=D,
                                    pattern=[[-P, KT], [D, NH]], channel_multiplier=-1).then_inc(mask_made, 1)
            nc.gpsimd.memset(ones_row[:, :], 1.0).then_inc(mask_made, 1)
            pool.wait_ge(mask_made, 2)
            nc.gpsimd.memset(ones_row[:, NK:P], 0.0).then_inc(mask_made, 1)
            nc.gpsimd.memset(sel[:, :, :], 1.0).then_inc(sel_made, 1)
            pool.wait_ge(sel_made, 1)
            for n, (i, c) in enumerate(pairs):
                base = (CAD - 1) * P * i - (S - 1) * P * c
                nc.gpsimd.affine_select(out=sel[:, n, :], in_=sel[:, n, :], compare_op=ALU.is_ge, fill=0.0, base=base,
                                        pattern=[[CAD - 1, P]], channel_multiplier=-(S - 1)).then_inc(sel_made, 1)
            pool.wait_ge(sel_made, 1 + len(pairs))
            for n, (i, c) in enumerate(pairs):
                base = (CAD - 1) * P * i - (S - 1) * P * c
                nc.gpsimd.affine_select(out=sel[:, n, :], in_=sel[:, n, :], compare_op=ALU.is_gt, fill=0.0,
                                        base=(S - 1) - base, pattern=[[-(CAD - 1), P]],
                                        channel_multiplier=S - 1).then_inc(sel_made, 1)
            with pool.Fori(0, B) as b:
                def key_stack(s, kt, k):
                    nc.gpsimd.tensor_tensor(gk[:, k, :], gT[:, s, bass.ds(kt * P, P)].bitcast(F32),
                                            one[:, 0:1].broadcast_to([P, P]), ALU.mult).then_inc(gk_made, 1)

                def x_low(kt, k):
                    pool.wait_ge(xh_made, b * 2 * TILES + kt + 1)
                    nc.gpsimd.tensor_tensor(xb_half(mm_lo)[:, k, :], xb[:, k].rearrange("p r d -> p (r d)"),
                                            xb_half(mm_hi)[:, k, :].bitcast(F32), ALU.subtract).then_inc(xl_made, 1)

                def low3(kt):
                    pool.wait_ge(eh3_made, b * 2 * TILES + kt + 1)
                    nc.gpsimd.tensor_tensor(e_half(mm_lo)[:, R - 1, :], e[:, R - 1, :], e_half(mm_hi)[:, R - 1, :].bitcast(F32),
                                            ALU.subtract).then_inc(elo3_made, 1)

                pool.wait_ge(gT_made, (b + 1) * TILES)
                key_stack(0, 0, 0)
                key_stack(0, 1, 1)
                x_low(0, 0)
                for s in range(SETS):
                    at = s * TILES

                    def step(kt, k, first=False, last=False):
                        if not (first and s == 0 and k < 2):
                            pool.wait_ge(sT_ps, b * 128 + at * 4 + kt * 4 + (4 * k - 4))
                        if last and k >= 2:
                            if s + 1 < SETS:
                                key_stack(s + 1, k - 2, k - 2)
                        else:
                            key_stack(s, kt + (k + 2), (k + 2) % 4)
                        if not (last and k == 3 and s + 1 == SETS):
                            x_low(kt + (at + k + 1), (k + 1) % 4)
                        low3(kt + (at + k))
                    for k in range(4):
                        step(0, k, first=True)
                    with pool.Fori(1, TILES // 4 - 1) as nkt:
                        kt = nkt * 4
                        for k in range(4):
                            step(kt, k)
                    for k in range(4):
                        step(TILES - 4, k, last=True)
                pool.wait_ge(rinv_made, (b + 1) * TILES)
                pool.wait_ge(s2_ps, b + 1)
                def normalise(i, u, first=False):
                    nc.gpsimd.tensor_tensor(probs[:, u, :, 0:NK], ex[:, bass.ds(i, 1)].rearrange("p a h k -> p (a h) k"),
                                            rinv[:, bass.ds(i, 1), :].rearrange("p a h -> p (a h)").unsqueeze(2)
                                            .broadcast_to([P, NH, NK]), ALU.mult)
                    if first:
                        pool.wait_ge(p2x_made, b + 1)
                    nc.gpsimd.tensor_tensor(probs[:, u, :, NK:P], p2x[:, bass.ds(i, 1)].rearrange("p a h k -> p (a h) k"),
                                            one[:, 0:1].unsqueeze(2).broadcast_to([P, NH, NT]), ALU.mult).then_inc(probs_made, 1)
                normalise(0, 0, True)
                normalise(1, 1)
                with pool.Fori(1, TILES // 2) as ni:
                    i = ni * 2
                    for u in range(2):
                        pool.wait_ge(pT_ps, b * TILES + i + (u - 1))
                        normalise(i + u, u)

        @block.scalar
        def _(act):
            for h in range(NH):
                act.wait_ge(wqT_ps, h + 1)
                nc.scalar.activation(wh[0:D, h, :], flat(2 * (h % 2))[0:D, 0:H], ACT.Copy).then_inc(wqT_made, 1)
            with act.Fori(0, B) as b:
                for n in range(KT * SETS):
                    act.wait_ge(mm_ps, b * KT * SETS + n + 1)
                    nc.scalar.activation(mm(mm_hi)[:, n // 2, n % 2, 0:SW].rearrange("p (r k) -> p r k", r=R),
                                         PS[:, n % 4, :].rearrange("p (r k) -> p r k", r=R)[:, :, 0:NK],
                                         ACT.Copy).then_inc(mmh_made, 1)
                act.wait_ge(aTm_ps, b + 1)
                act.wait_ge(aTm_zero, b + 1)
                for r in range(R):
                    nc.scalar.activation(aTm[r * SLOTS:r * SLOTS + 16, r, :], PS[r * SLOTS:r * SLOTS + 16, 2, 0:CAD],
                                         ACT.Copy).then_inc(aTm_made, 1)

                def xT(i, u, ring=True):
                    act.wait_ge(xT_ps, b * TILES + i + 1)
                    if ring:
                        act.wait_ge(sc_ps, b * TILES + i + (-1))
                    nc.scalar.activation(xT_hi[:, u].rearrange("p k n -> p (k n)"), flat(0)[:, 0:H],
                                         ACT.Copy).then_inc(xTh_made, 1)

                def soft(i, u):
                    act.wait_ge(negmax_made, b * TILES + i + 1)
                    for h in range(NH):
                        last = nc.scalar.activation(
                            ex[:, bass.ds(i, 1), h, :].rearrange("p a k -> p (a k)"),
                            scores_of(u)[:, h // R, (h % R) * NK:(h % R + 1) * NK], ACT.Exp,
                            bias=negmax[:, u, h:h + 1], scale=SCALE, accum_out=sums[:, u, h:h + 1])
                    last.then_inc(exp_made, 1)

                def g(i):
                    act.wait_ge(gT_ps, b * TILES + i + 1)
                    nc.scalar.activation(gT[:, :, bass.ds(i * P, P)], PS[:, 1, P:P + SETS * P].rearrange("p (s n) -> p s n", s=SETS),
                                         ACT.Copy).then_inc(gT_made, 1)

                xT(0, 0, False)
                xT(1, 1, False)
                xT(2, 0)
                soft(0, 0)
                g(0)
                xT(3, 1)
                soft(1, 1)
                g(1)
                with act.Fori(1, TILES // 2 - 1) as ni:
                    i = ni * 2
                    for u in range(2):
                        xT(i + (u + 2), u)
                        soft(i + u, u)
                        g(i + u)
                soft(TILES - 2, 0)
                g(TILES - 2)
                g(TILES - 1)
                soft(TILES - 1, 1)
                for s in range(SETS):
                    act.wait_ge(aT_ps, b * SETS + 1 + s)
                    nc.scalar.activation(aT[:, s, :], PS[:, s, 0:CAD], ACT.Copy).then_inc(aT_made, 1)
                def x_high(kt, k):
                    act.wait_ge(xb_in[k], b * 128 + (kt - k) * 4 + 16)
                    nc.scalar.activation(xb_half(mm_hi)[:, k, :], xb[:, k].rearrange("p r d -> p (r d)"), ACT.Copy)\
                        .then_inc(xh_made, 1)

                def key_exps(kt):
                    for r in range(R):
                        act.wait_ge(sT_ps, b * 128 + kt * 4 + (r + 1))
                        nc.scalar.activation(e[:, r, :], PS[:, 4 + r, 0:CAD], ACT.Exp, scale=SCALE).then_inc(e_made, 1)
                    nc.scalar.activation(e_half(mm_hi)[:, R - 1, :], PS[:, 3 + R, 0:CAD], ACT.Exp, scale=SCALE).then_inc(eh3_made, 1)
                x_high(0, 0)
                for s in range(SETS):
                    at = s * TILES
                    with act.Fori(0, TILES // 4 - 1) as nkt:
                        kt = nkt * 4
                        for k in range(4):
                            x_high(kt + (at + k + 1), (k + 1) % 4)
                            key_exps(kt + (at + k))
                    for k in range(4):
                        if k < 3 or s + 1 < SETS:
                            x_high(at + TILES - 3 + k, (k + 1) % 4)
                        key_exps(at + TILES - 4 + k)
                    for r in (0, 2):
                        act.wait_ge(pv_done, b * 128 + s * 64 + (61 + r))
                        nc.scalar.activation(nsum_of(s * R + r), PS[0:D + 1, r, 0:CAD], ACT.Copy).then_inc(nsa_made, 1)

                def vw_high(*ns):
                    for n in ns:
                        act.wait_ge(vw_ps, b * 2 * NH + n + 1)
                        nc.scalar.activation(vw(mm_hi)[:, n // 2, n % 2, :], PS[:, 6 + n % 2, 0:HALF], ACT.Copy).then_inc(vwh_made, 1)

                def hT(c):
                    act.wait_ge(hT_ps, b * CT + c + 1)
                    nc.scalar.activation(hs1T[:, c].rearrange("p k n -> p (k n)"), flat((4, 2, 4)[c])[:, 0:H],
                                         ACT.Copy).then_inc(hT_made, 1)
                vw_high(0, 1, 2, 3)
                hT(0)
                vw_high(4, 5)
                hT(1)
                vw_high(6, 7)
                hT(2)
                vw_high(8, 9, 10, 11)
                act.wait_ge(s2_made, b + 1)
                nc.scalar.activation(e2[:, :, :], s2[:, :, :], ACT.Exp, scale=SCALE).then_inc(e2_made, 1)
                vw_high(12, 13, 14, 15)

                def pT(i, u, ring=True):
                    act.wait_ge(pT_ps, b * TILES + i + 1)
                    if ring:
                        act.wait_ge(out_ps, b * TILES + i + (-1))
                    nc.scalar.activation(pT_hi[:, u].rearrange("p h n -> p (h n)"), flat(2 * u), ACT.Copy).then_inc(pTh_made, 1)
                pT(0, 0, False)
                pT(1, 1, False)
                with act.Fori(1, TILES // 2) as ni:
                    i = ni * 2
                    for u in range(2):
                        pT(i + u, u)

        @block.vector
        def _(dve):
            nc.vector.memset(gs[:, :, :, :], 0.0).then_inc(gs_set, 1)
            nc.vector.memset(as_[:, :, :, :], 0.0).then_inc(gs_set, 1)
            nc.vector.memset(xb[:, :, :, :], 1.0).then_inc(gs_set, 1)
            nc.vector.memset(res[:, :, :], 0.0).then_inc(res_made, 1)
            nc.vector.memset(mpart[:, :, :], 0.0).then_inc(mx_made, 1)
            nc.vector.memset(mraw[:, :, :], 0.0).then_inc(mx_made, 1)
            dve.wait_ge(gs_set, 1)
            nc.vector.memset(gs[:, :, :, 16:18], 1.0).then_inc(gs_set, 1)
            dve.wait_ge(wca_ps, 1)
            dve.wait_ge(mask_made, 3)
            for j in range(KT):
                last = nc.vector.tensor_tensor(wca[:, j], PS[:, 0, j * NT:(j + 1) * NT].unsqueeze(1).broadcast_to([P, NH, NT]),
                                               headmask[:, j, :].unsqueeze(2).broadcast_to([P, NH, NT]), ALU.mult)
            last.then_inc(wca_made, 1)
            dve.wait_ge(ctxT_ps, 1)
            nc.vector.tensor_copy(ctxT[:, :, :, :].rearrange("p c b n -> p (c b n)"), flat(4)[:, 0:B * CAD]).then_inc(ctxT_made, 1)
            dve.wait_ge(ctxT_made, 1)
            nc.vector.tensor_copy(caT[:, :, :, :], ctxT[:, :, :, NK:P].rearrange("p c b t -> p b c t")).then_inc(caT_made, 1)
            for h in range(NH):
                dve.wait_ge(kv_ps, h + 1)
                for b, to in enumerate((kv, kv_next)):
                    nc.vector.tensor_copy(to[0:D, h], PS[0:D, 4 + h % 4, :].rearrange("p (a b n) -> p a b n", a=2, b=B)[:, :, b, :])\
                        .then_inc(kv_made, 1)
            with dve.Fori(0, B) as b:
                nc.vector.memset(aTm[:, :, :].bitcast(F32), 0.0).then_inc(aTm_zero, 1)
                dve.wait_ge(caT_made, 1)
                dve.wait_ge(gs_set, 4)

                def as_half(c, lo):
                    return as_[:, c, :, 0:16].rearrange("p h (a l t) -> p h a l t", a=2, l=2)[:, :, :, lo, :]

                def ca(c):
                    return caT[:, bass.ds(b, 1), c, :].rearrange("p a t -> p (a t)").unsqueeze(1).unsqueeze(1)\
                        .broadcast_to([P, NH, 2, NT])
                for c in range(CT):
                    nc.vector.tensor_copy(as_half(c, 0).bitcast(F32R), ca(c)).then_inc(as_hi, 1)
                dve.wait_ge(as_hi, (b + 1) * CT)
                for c in range(CT):
                    nc.vector.tensor_tensor(as_half(c, 1).bitcast(F32R), ca(c), as_half(c, 0), ALU.subtract).then_inc(as_made, 1)
                dve.wait_ge(wca_made, 1)
                for n in range(KT * SETS):
                    j, s = n // 2, n % 2
                    ps = PS[:, n % 4, :].rearrange("p (r k) -> p r k", r=R)
                    dve.wait_ge(mmh_made, b * KT * SETS + n + 1)
                    nc.vector.tensor_tensor(mm(mm_lo)[:, j, s, 0:SW].rearrange("p (r k) -> p r k", r=R), ps[:, :, 0:NK],
                                            mm(mm_hi)[:, j, s, 0:SW].bitcast(F32).rearrange("p (r k) -> p r k", r=R), ALU.subtract)
                    nc.vector.tensor_copy(wk2[:, j, s * R:(s + 1) * R, :], ps[:, :, NK:P]).then_inc(mml_made, 1)
                for s in range(SETS):
                    nc.vector.tensor_copy(mm(mm_hi)[:, :, s, SW:BANK], wca[:, :, s * R:(s + 1) * R, :].rearrange("p k r t -> p k (r t)"))\
                        .then_inc(mml_made, 1)
                dve.wait_ge(mml_made, b * 14 + 12)
                for s in range(SETS):
                    nc.vector.tensor_tensor(mm(mm_lo)[:, :, s, SW:BANK], wca[:, :, s * R:(s + 1) * R, :].rearrange("p k r t -> p k (r t)"),
                                            mm(mm_hi)[:, :, s, SW:BANK].bitcast(F32), ALU.subtract).then_inc(mml_made, 1)

                def xT(i, u):
                    dve.wait_ge(xTh_made, b * TILES + i + 1)
                    nc.vector.tensor_tensor(xT_lo[:, u].rearrange("p k n -> p (k n)"), flat(0)[:, 0:H],
                                            xT_hi[:, u].bitcast(F32).rearrange("p k n -> p (k n)"), ALU.subtract).then_inc(xTl_made, 1)

                def gs_half(u, s, lo):
                    return gs[:, u, s * R:(s + 1) * R, 8 * lo:8 * lo + 8].rearrange("p r (a t) -> p r a t", a=2)

                def g_rep(u, s):
                    return g_of(u)[:, s].unsqueeze(2).broadcast_to([P, R, 2, NT])

                def soft(i, u, first=False):
                    dve.wait_ge(sc_ps, b * TILES + i + 1)
                    if not first:
                        dve.wait_ge(exp_made, b * TILES + i + (-1))
                    nc.vector.tensor_reduce(top[:, u, :].rearrange("p (s r) -> p s r", s=SETS), scores_of(u)[:, :, 0:SW].rearrange("p s (r k) -> p s r k", r=R),
                                            AX.X, ALU.max).then_inc(top_made, 1)
                    if not first:
                        dve.wait_ge(gT_ps, b * TILES + i + (-1))
                    for s in range(SETS):
                        nc.vector.tensor_copy(gs_half(u, s, 0).bitcast(F32R), g_rep(u, s)).then_inc(gs_hi, 1)
                    dve.wait_ge(gs_hi, b * 2 * TILES + i * 2 + 2)
                    for s in range(SETS):
                        last = nc.vector.tensor_tensor(gs_half(u, s, 1).bitcast(F32R), g_rep(u, s), gs_half(u, s, 0), ALU.subtract)
                    last.then_inc(gs_made, 1)
                    dve.wait_ge(top_made, b * TILES + i + 1)
                    dve.wait_ge(gs_made, b * TILES + i + 1)
                    nc.vector.tensor_scalar(negmax[:, u, :], top[:, u, :], -SCALE, None, ALU.mult).then_inc(negmax_made, 1)

                def inv(i, u):
                    dve.wait_ge(exp_made, b * TILES + i + 1)
                    nc.vector.reciprocal(rinv[:, bass.ds(i, 1), :].rearrange("p a h -> p (a h)"), sums[:, u, :]).then_inc(rinv_made, 1)

                def units(chunk, half):
                    for p in range(half * UNITS // 2, (half + 1) * UNITS // 2):
                        dve.wait_ge(mx_ps, b * MXB + chunk * UNITS + p + 1)
                        nc.vector.tensor_reduce(mpart[:, bass.ds(chunk, 1), 2 * p:2 * p + 2].rearrange("p a n -> p (a n)"),
                                                PS[:, 2 + p % 2, :].rearrange("p (h n) -> p h n", h=2), AX.X, ALU.max).then_inc(mx_made, 1)

                dve.wait_ge(mx_made, 2)
                xT(0, 0)
                xT(1, 1)
                xT(2, 0)
                soft(0, 0, True)
                inv(0, 0)
                xT(3, 1)
                soft(1, 1, True)
                inv(1, 1)
                xT(4, 0)
                soft(2, 0)
                inv(2, 0)
                with dve.Fori(2, TILES // 2 - 1) as ni:
                    i = ni * 2
                    for u in range(2):
                        xT(i + (u + 1), 1 - u)
                        soft(i + (u - 1), 1 - u)
                        units(ni + (-2), u)
                        inv(i + (u - 1), 1 - u)
                xT(TILES - 1, 1)
                soft(TILES - 3, 1)
                units(CHUNKS - 1, 0)
                inv(TILES - 3, 1)
                soft(TILES - 2, 0)
                units(CHUNKS - 1, 1)
                inv(TILES - 2, 0)
                soft(TILES - 1, 1)
                for p in range(UNITS):
                    dve.wait_ge(mx_ps, b * MXB + CHUNKS * UNITS + p + 1)
                    nc.vector.tensor_reduce(mpart[:, CHUNKS, 2 * p:2 * p + 2], PS[:, 2 + 2 * (p % 3):4 + 2 * (p % 3), :],
                                            AX.X, ALU.max).then_inc(mx_made, 1)
                inv(TILES - 1, 1)
                dve.wait_ge(mx_made, 2 + (b + 1) * MXB)
                nc.vector.tensor_reduce(mraw[:, :, :].rearrange("p c h -> p (c h)"), mpart[:, :, :].rearrange("p k n -> p n k"),
                                        AX.X, ALU.max).then_inc(mpart_made, 1)
                dve.wait_ge(mpart_made, b + 1)
                nc.vector.tensor_scalar(as_[:, :, :, 16].bitcast(F32R), mraw[:, :, :], -1.0, None, ALU.mult).then_inc(asm_hi, 1)
                dve.wait_ge(asm_hi, b + 1)
                nc.vector.scalar_tensor_tensor(as_[:, :, :, 17].bitcast(F32R), mraw[:, :, :], -1.0, as_[:, :, :, 16],
                                               ALU.mult, ALU.subtract).then_inc(asm_made, 1)
                for s in range(SETS):
                    with dve.Fori(0, TILES) as kt:
                        for r in range(R - 1):
                            dve.wait_ge(e_made, b * 128 + s * 64 + kt * 4 + (r + 1))
                            nc.vector.tensor_copy(e_half(mm_hi)[:, r, :], e[:, r, :]).then_inc(ehi_made, 1)
                            dve.wait_ge(ehi_made, b * 96 + s * 48 + kt * 3 + (r + 1))
                            nc.vector.tensor_tensor(e_half(mm_lo)[:, r, :], e[:, r, :], e_half(mm_hi)[:, r, :].bitcast(F32),
                                                    ALU.subtract).then_inc(elo_made, 1)
                    for r in (1, 3):
                        dve.wait_ge(pv_done, b * 128 + s * 64 + (61 + r))
                        nc.vector.tensor_copy(nsum_of(s * R + r), PS[0:D + 1, r, 0:CAD]).then_inc(nsd_made, 1)

                def vw_low(*ns):
                    for n in ns:
                        dve.wait_ge(vwh_made, b * 2 * NH + n + 1)
                        nc.vector.tensor_tensor(vw(mm_lo)[:, n // 2, n % 2, :], PS[:, 6 + n % 2, 0:HALF],
                                                vw(mm_hi)[:, n // 2, n % 2, :].bitcast(F32), ALU.subtract).then_inc(vwl_made, 1)

                def value_rows(c):
                    at = (0, 2, 0)[c]
                    ps = PS[:, at:at + 2, 0:R * (D + 1)].rearrange("p s (r d) -> p s r d", r=R)
                    dve.wait_ge(nT_ps, b * CT + c + 1)
                    nc.vector.reciprocal(rl[:, c, :].rearrange("p (s r) -> p s r", s=SETS), ps[:, :, :, D]).then_inc(rl_made, 1)
                    dve.wait_ge(rl_made, b * CT + c + 1)
                    for s in range(SETS):
                        last = nc.vector.tensor_tensor(hs1[:, c, s * R:(s + 1) * R, :], ps[:, s, :, 0:D],
                                                       rl[:, c, s * R:(s + 1) * R].unsqueeze(2).broadcast_to([P, R, D]), ALU.mult)
                    last.then_inc(hs1_made, 1)
                vw_low(0, 1)
                value_rows(0)
                value_rows(1)
                vw_low(2, 3)
                value_rows(2)
                vw_low(4, 5, 6, 7, 8, 9)
                dve.wait_ge(s2_ps, b + 1)
                sc2 = PS[:, 0, 0:CT * NH * NT].rearrange("p (g t) -> p g t", t=NT)
                nc.vector.tensor_reduce(m2[:, :], sc2, AX.X, ALU.max).then_inc(m2_made, 1)
                dve.wait_ge(m2_made, b + 1)
                nc.vector.tensor_tensor(s2[:, :, :], sc2, m2[:, :].unsqueeze(2).broadcast_to([P, CT * NH, NT]), ALU.subtract).then_inc(s2_made, 1)
                vw_low(10, 11)
                dve.wait_ge(e2_made, b + 1)
                nc.vector.tensor_reduce(l2[:, :], e2[:, :, :], AX.X, ALU.add).then_inc(l2_made, 1)
                dve.wait_ge(l2_made, b + 1)
                nc.vector.reciprocal(r2[:, :], l2[:, :]).then_inc(r2_made, 1)
                dve.wait_ge(r2_made, b + 1)
                nc.vector.tensor_tensor(p2[:, :, :].rearrange("p c (h t) -> p (c h) t", t=NT), e2[:, :, :],
                                        r2[:, :].unsqueeze(2).broadcast_to([P, CT * NH, NT]), ALU.mult).then_inc(p2_made, 1)
                vw_low(12, 13)
                dve.wait_ge(p2x_ps, b + 1)
                nc.vector.tensor_copy(p2x[:, :, :, :].rearrange("p i h t -> p (i h t)"), PS[:, 1, :]).then_inc(p2x_made, 1)
                vw_low(14, 15)

                def pT(i, u):
                    dve.wait_ge(pTh_made, b * TILES + i + 1)
                    nc.vector.tensor_tensor(pT_lo[:, u].rearrange("p h n -> p (h n)"), flat(2 * u),
                                            pT_hi[:, u].bitcast(F32).rearrange("p h n -> p (h n)"), ALU.subtract).then_inc(pTl_made, 1)

                def add_x(i, u):
                    dve.wait_ge(out_ps, b * TILES + i + 1)
                    dve.wait_ge(x_in[u], b * TILES * 16 + (TILES // 2 + 1) * 16 + (i - u) * 8)
                    dve.wait_ge(stored[u], 16 + b * (TILES // 2) * 16 + (i - u) * 8)
                    nc.vector.tensor_tensor(res[:, u, :].rearrange("p (f n) -> p f n", f=2), PS[:, 4 + 2 * u:6 + 2 * u, 0:HALF],
                                            xin[:, u, :].rearrange("p (f n) -> p f n", f=2), ALU.add).then_inc(res_made, 1)
                pT(0, 0)
                with dve.Fori(0, TILES // 2 - 1) as ni:
                    i = ni * 2
                    for u in range(2):
                        pT(i + (u + 1), 1 - u)
                        add_x(i + u, u)
                pT(TILES - 1, 1)
                add_x(TILES - 2, 0)
                add_x(TILES - 1, 1)

        @block.tensor
        def _(pe):
            mul = nc.tensor.matmul
            pe.wait_ge(stored[0], 16)
            pe.wait_ge(ident_made, 1)
            for j in range(KT):
                last = nc.tensor.transpose(PS[:, 0, j * NT:(j + 1) * NT], wqca_in[:, j * P:(j + 1) * P], ident[0:NT, 0:NT])
            last.then_inc(wca_ps, 1)
            pe.wait_ge(wca_made, 1)
            pe.wait_ge(wq_in_s, 16)
            for h in range(NH):
                if h >= 2:
                    pe.wait_ge(wqT_made, h - 1)
                for j in range(KT):
                    last = nc.tensor.transpose(flat(2 * (h % 2))[0:D, j * P:(j + 1) * P], wq_in[:, j, h * D:(h + 1) * D], ident[:, :])
                last.then_inc(wqT_ps, 1)
            pe.wait_ge(ctx_in_s, 16)
            for c in range(CT):
                for b in range(B):
                    last = nc.tensor.transpose(flat(4)[:, (c * B + b) * P:(c * B + b + 1) * P], ctx_tok[:, b, c * P:(c + 1) * P],
                                               ident[:, :])
            last.then_inc(ctxT_ps, 1)
            pe.wait_ge(ctxT_made, 1)
            for h in range(NH):
                if h >= 4:
                    pe.wait_ge(kv_made, 2 * (h - 3))
                for a in range(2):
                    pe.wait_ge(wkv_in_s[a], 32)
                    ps = PS[0:D, 4 + h % 4, a * B * P:(a + 1) * B * P].rearrange("p (b n) -> p b n", b=B)
                    for w, t0, t1 in ((2 * a, 0, NK), (2 * a + 1, NK, P)):
                        for c in range(CT):
                            last = mul(ps[:, :, t0:t1], wkv_in[:, w, c, h * D:(h + 1) * D], ctxT[:, c, :, t0:t1],
                                       start=(c == 0), stop=(c == CT - 1))
                last.then_inc(kv_ps, 1)
            pe.wait_ge(stored[1], 16)
            pe.wait_ge(kv_made, 2 * NH)
            pe.wait_ge(wqT_made, NH)
            with pe.Fori(0, B) as b:
                pe.wait_ge(reload_in, 16 + b * 32)
                for n in range(KT * SETS):
                    if n >= 4:
                        pe.wait_ge(mml_made, b * 14 + n - 3)
                    for r in range(R):
                        h = (n % 2) * R + r
                        last = mul(PS[:, n % 4, r * P:(r + 1) * P], wh[0:D, h, (n // 2) * P:(n // 2 + 1) * P], kv[0:D, h, 0, :],
                                   start=True, stop=True)
                    last.then_inc(mm_ps, 1)
                pe.wait_ge(mml_made, (b + 1) * 14)
                pe.wait_ge(as_made, (b + 1) * CT)
                for c in range(CT):
                    last = nc.tensor.transpose(PS[:, 2, c * P:(c + 1) * P], as_[:, c, 0:R, :].rearrange("p r n -> p (r n)"), ident[:, :])
                last.then_inc(aTm_ps, 1)

                def xT(i, u, first=False):
                    pe.wait_ge(x_in[u], b * TILES * 16 + (i - u) * 8 + 16)
                    if not first:
                        pe.wait_ge(gT_made, b * TILES + i + (-2))
                    for j in range(KT):
                        last = nc.tensor.transpose(flat(0)[:, j * P:(j + 1) * P], xin[:, u, j * P:(j + 1) * P], ident[:, :])
                    last.then_inc(xT_ps, 1)

                def pair_scores(chunk, p):
                    pe.wait_ge(mx_made, b * MXB + chunk * UNITS + (p + 1))
                    c, h = 2 * p // NH, 2 * p % NH
                    for k in range(2):
                        last = mul(PS[:, 2 + p % 2, k * 2 * P:(k + 1) * 2 * P], aTm[:, (h + k) % R, c * P:(c + 1) * P],
                                   gT[:, h // R, bass.ds(chunk * 2 * P, 2 * P)], start=True, stop=True)
                    last.then_inc(mx_ps, 1)

                def step(i, u, next_x=True, first=False, g=True, g_first=False, chunk=None):
                    if next_x:
                        xT(i + 1, 1 - u)
                    pe.wait_ge(xTl_made, b * TILES + i + 1)
                    if not first:
                        pe.wait_ge(exp_made, b * TILES + i + (-1))
                    done = 0
                    p = u * UNITS // 2
                    for j in range(KT):
                        for n, (l, rr) in enumerate(((xT_hi, mm_hi), (xT_hi, mm_lo), (xT_lo, mm_hi))):
                            for s in range(SETS):
                                last = mul(scores_of(u)[:, s, :], l[:, u, j, :], mm(rr)[:, j, s, :],
                                           start=(j == 0 and n == 0), stop=(j == KT - 1 and n == 2))
                                done += 1
                                if g and done == 20:
                                    if next_x:
                                        pe.wait_ge(xTl_made, b * TILES + i + 2)
                                    g_stack(i + (-1), 1 - u, first=g_first)
                                if chunk is not None and done >= 14 and (done - 14) % 3 == 0 and done < 30:
                                    pair_scores(chunk, p)
                                    p += 1
                    last.then_inc(sc_ps, 1)
                    assert chunk is None or p == (u + 1) * UNITS // 2

                def g_stack(i, u, first=False):
                    if not first:
                        pe.wait_ge(gT_made, b * TILES + i)
                    pe.wait_ge(gs_made, b * TILES + i + 1)
                    for s in range(SETS):
                        last = nc.tensor.transpose(PS[:, 1, P + s * P:P + (s + 1) * P],
                                                   gs[:, u, s * R:(s + 1) * R, :].rearrange("p r n -> p (r n)"), ident[:, :])
                    last.then_inc(gT_ps, 1)

                xT(0, 0, True)
                pe.wait_ge(xTl_made, b * TILES + 1)
                xT(1, 1, True)
                step(0, 0, False, True, False)
                pe.wait_ge(xTl_made, b * TILES + 2)
                xT(2, 0, True)
                step(1, 1, False, True, g_first=True)
                step(2, 0)
                pe.wait_ge(aTm_made, (b + 1) * R)
                step(3, 1)
                with pe.Fori(2, TILES // 2 - 1) as ni:
                    i = ni * 2
                    for u in range(2):
                        step(i + u, u, chunk=ni + (-2))
                step(TILES - 2, 0, chunk=CHUNKS - 1)
                step(TILES - 1, 1, next_x=False, chunk=CHUNKS - 1)
                g_stack(TILES - 1, 1)

                pe.wait_ge(gT_made, (b + 1) * TILES)
                for p in range(UNITS):
                    if p == 0:
                        pe.wait_ge(mx_made, 2 + b * MXB + CHUNKS * UNITS)
                    elif p == 2:
                        pe.wait_ge(exp_made, (b + 1) * TILES)
                    elif p >= 3:
                        pe.wait_ge(mx_made, b * MXB + CHUNKS * UNITS + p)
                    c, h = 2 * p // NH, 2 * p % NH
                    for k in range(2):
                        last = mul(PS[:, 2 + 2 * (p % 3) + k, :], aTm[:, (h + k) % R, c * P:(c + 1) * P],
                                   gT[:, h // R, S - BANK:S], start=True, stop=True)
                    last.then_inc(mx_ps, 1)
                pe.wait_ge(asm_made, b + 1)
                for s in range(SETS):
                    for c in range(CT):
                        last = nc.tensor.transpose(PS[:, s, c * P:(c + 1) * P],
                                                   as_[:, c, s * R:(s + 1) * R, :].rearrange("p r n -> p (r n)"), ident[:, :])
                    last.then_inc(aT_ps, 1)
                pe.wait_ge(aT_made, (b + 1) * SETS)
                def sT(s, kt, k, r):
                    if r == 0:
                        pe.wait_ge(gk_made, b * 2 * TILES + s * TILES + kt + 1)
                    mul(PS[:, 4 + r, 0:CAD], gk[r * SLOTS:r * SLOTS + 18, k, :], aT[r * SLOTS:r * SLOTS + 18, s, :],
                        start=True, stop=True).then_inc(sT_ps, 1)

                def pv(s, kt, k, r, start=False, stop=False):
                    if r == 0:
                        pe.wait_ge(xl_made, b * 2 * TILES + s * TILES + kt + 1)
                    if r < R - 1:
                        pe.wait_ge(elo_made, b * 96 + s * 48 + kt * 3 + (r + 1))
                    else:
                        pe.wait_ge(elo3_made, b * 2 * TILES + s * TILES + kt + 1)
                    for n, (xx, ee) in enumerate(((mm_hi, mm_hi), (mm_lo, mm_hi), (mm_hi, mm_lo))):
                        last = mul(PS[0:D + 1, r, 0:CAD], xb_half(xx)[:, k, r * (D + 1):(r + 1) * (D + 1)], e_half(ee)[:, r, :],
                                   start=(start and n == 0), stop=(stop and n == 2))
                    last.then_inc(pv_done, 1)

                for r in range(R):
                    sT(0, 0, 0, r)
                for s in range(SETS):
                    for kt in range(4):
                        for r in range(R):
                            if s and kt == 0:
                                if r % 2:
                                    pe.wait_ge(nsd_made, b * R + (r + 1) // 2)
                                else:
                                    pe.wait_ge(nsa_made, b * R + r // 2 + 1)
                            pv(s, kt, kt, r, start=(kt == 0))
                            sT(s, kt + 1, (kt + 1) % 4, r)
                    with pe.Fori(1, TILES // 4 - 1) as nkt:
                        kt = nkt * 4
                        for k in range(4):
                            for r in range(R):
                                pv(s, kt + k, k, r)
                                sT(s, kt + (k + 1), (k + 1) % 4, r)
                    for k in range(4):
                        for r in range(R):
                            pv(s, TILES - 4 + k, k, r, stop=(k == 3))
                            if k < 3:
                                sT(s, TILES - 3 + k, k + 1, r)
                            elif s + 1 < SETS:
                                sT(s + 1, 0, 0, r)

                def vw_product(*ns):
                    for n in ns:
                        h, f = n // 2, n % 2
                        if n >= 2:
                            pe.wait_ge(vwl_made, b * 2 * NH + n - 1)
                        rows = D + 1 if h == 0 else D
                        mul(PS[:, 6 + n % 2, 0:HALF], kv[0:rows, h, 1, :], wh[0:rows, h, f * HALF:(f + 1) * HALF],
                            start=True, stop=True).then_inc(vw_ps, 1)

                def sums_T(c):
                    for h in range(NH):
                        at = (h % R) * (D + 1)
                        last = nc.tensor.transpose(PS[:, (0, 2, 0)[c] + h // R, at:at + D + 1], nsum_of(h)[:, c * P:(c + 1) * P],
                                                   ident[0:D + 1, 0:D + 1])
                    last.then_inc(nT_ps, 1)

                def values_T(c):
                    pe.wait_ge(hs1_made, b * CT + c + 1)
                    for j in range(KT):
                        last = nc.tensor.transpose(flat((4, 2, 4)[c])[:, j * P:(j + 1) * P],
                                                   hs1[:, c].rearrange("p h d -> p (h d)")[:, j * P:(j + 1) * P], ident[:, :])
                    last.then_inc(hT_ps, 1)
                pe.wait_ge(wout_in_s, (b + 1) * 32)
                vw_product(0, 1)
                pe.wait_ge(nsa_made, (b + 1) * R)
                pe.wait_ge(nsd_made, (b + 1) * R)
                sums_T(0)
                sums_T(1)
                vw_product(2, 3)
                pe.wait_ge(hs1_made, b * CT + 1)
                sums_T(2)
                values_T(0)
                vw_product(4, 5)
                values_T(1)
                vw_product(6, 7)
                pe.wait_ge(hT_made, b * CT + 1)
                values_T(2)
                vw_product(8, 9)
                for c in range(CT):
                    pe.wait_ge(hT_made, b * CT + c + 1)
                    for j in range(KT):
                        last = mul(PS[:, 0, c * 32:(c + 1) * 32], hs1T[:, c, j, :], wk2[:, j].rearrange("p h t -> p (h t)"),
                                   start=(j == 0), stop=(j == KT - 1))
                last.then_inc(s2_ps, 1)
                vw_product(10, 11, 12)
                pe.wait_ge(sel_made, 1 + 2 * len(pairs))
                pe.wait_ge(p2_made, b + 1)
                for n, (i, c) in enumerate(pairs):
                    last = mul(PS[:, 1, i * 32:(i + 1) * 32], sel[:, n, :], p2[:, c, :],
                               start=(n == 0 or pairs[n - 1][0] != i), stop=(n + 1 == len(pairs) or pairs[n + 1][0] != i))
                last.then_inc(p2x_ps, 1)
                vw_product(13, 14, 15)

                def pT(i, u, first=False):
                    pe.wait_ge(probs_made, b * TILES + i + 1)
                    if not first:
                        pe.wait_ge(pTl_made, b * TILES + i + (-1))
                    for h in range(NH):
                        last = nc.tensor.transpose(flat(2 * u)[:, h * P:(h + 1) * P], probs[:, u, h, :], ident[:, :])
                    last.then_inc(pT_ps, 1)

                def output(i, u, first=False):
                    pe.wait_ge(pTl_made, b * TILES + i + 1)
                    if not first:
                        pe.wait_ge(res_made, 1 + b * TILES + i + (-1))
                    for h in range(NH):
                        for n, (l, rr) in enumerate(((pT_hi, mm_hi), (pT_hi, mm_lo), (pT_lo, mm_hi))):
                            for f in range(2):
                                last = mul(PS[:, 4 + 2 * u + f, 0:HALF], l[:, u, h, :], vw(rr)[:, h, f, :],
                                           start=(h == 0 and n == 0), stop=(h == NH - 1 and n == 2))
                    last.then_inc(out_ps, 1)

                pe.wait_ge(p2x_made, b + 1)
                pT(0, 0, True)
                pT(1, 1, True)
                pe.wait_ge(vwl_made, (b + 1) * 2 * NH)
                output(0, 0, True)
                pT(2, 0)
                output(1, 1, True)
                with pe.Fori(1, TILES // 2 - 1) as ni:
                    i = ni * 2
                    for u in range(2):
                        pT(i + (u + 1), 1 - u)
                        output(i + u, u)
                pT(TILES - 1, 1)
                output(TILES - 2, 0)
                output(TILES - 1, 1)


_INS = ['x', 'ctx_768', 'L0_xattn_Wq', 'L0_xattn_Wk', 'L0_xattn_Wv', 'L0_xattn_Wq_ca', 'L0_xattn_Wk_ca', 'L0_xattn_Wv_ca',
        'L0_xattn_Wout', 'L0_xattn_b_out']


def kernel(**inputs):
    import concourse.bacc as bacc
    from concourse.bass_utils import run_bass_kernel_spmd as run

    nc = bacc.Bacc("TRN2", target_bir_lowering=False, num_devices=1)
    arrays, args = {}, []
    for name in _INS:
        a = np.ascontiguousarray(inputs[name])
        arrays[f"in_{name}"] = a
        args.append(nc.dram_tensor(f"in_{name}", a.shape, mybir.dt.from_np(a.dtype), kind="ExternalInput").ap())
    args.append(nc.dram_tensor("out_0", (B, S, H), F32, kind="ExternalOutput").ap())
    build(nc, *args)
    r = run(nc, [arrays], core_ids=[0])
    return r.results[0]["out_0"]
```

```python
import numpy as np
import concourse.bass as bass
from concourse import mybir
from contextlib import ExitStack

F32, F32R = mybir.dt.float32, mybir.dt.float32r
ALU, ACT, AX = mybir.AluOpType, mybir.ActivationFunctionType, mybir.AxisListType

P = 128
B, S, H = 2, 2048, 640
NH, D = 8, 80
CAD = 384
NT = 4
NK = P - NT
SCALE = float(D) ** -0.5
TILES = S // P
KT = H // P
CT = CAD // P
SETS, R = 2, 4
SW = R * NK
BANK = 512
SLOTS = 32
HALF = H // 2
CHUNKS = TILES // 2
ES = 2 * R
AHEAD = 6
UNITS = CT * NH // 2
HALVES = (range(UNITS // 2), range(UNITS // 2, UNITS))
VW_ORDER = [14, 15] + list(range(14))
RAW_AT = 2 * -(-KT * SETS * R * P // (2 * NH * NK))
RELOADS = 16 * (1 + KT)
MXB = CHUNKS * UNITS


def gather_pairs():
    index = np.linspace(0, CAD - 1, S).astype(np.int64)
    assert (index == (np.arange(S) * (CAD - 1)) // (S - 1)).all()
    return [(i, c) for i in range(TILES)
            for c in range(index[i * P] // P, index[i * P + P - 1] // P + 1)]


def build(nc, x, ctx_in, wq, wk, wv, wqca, wkca, wvca, wout, bout, out):
    pairs = gather_pairs()
    ctx = ExitStack()
    with ctx:
        def sb(name, shape, dt=F32):
            return ctx.enter_context(nc.sbuf_tensor(name, shape, dt))

        def sem(name):
            return ctx.enter_context(nc.semaphore(name))

        ident = sb("ident", [P, P])
        one = sb("one", [P, 1])
        headmask = sb("headmask", [P, KT, NH])
        wca = sb("wca", [P, KT, NH, NT])
        sel = sb("sel", [P, len(pairs), P])
        vT = sb("vT", [P, NH, P])
        wh = sb("wh", [P, NH, H])
        mm_hi = sb("mm_hi", [P, KT * SETS * BANK], F32R)
        mm_lo = sb("mm_lo", [P, KT * SETS * BANK], F32R)
        wk2 = sb("wk2", [P, KT, NH, NT])
        xin = sb("xin", [P, 2, H])
        xb = sb("xb", [P, 4, R, D + 1])
        negmax = sb("negmax", [P, 2, NH])
        top = sb("top", [P, 2, NH])
        sums = sb("sums", [P, 2, NH])
        rinv = sb("rinv", [P, TILES, NH])
        gs = sb("gs", [P, 2, NH, SLOTS])
        as_ = sb("as_", [P, CT, NH, SLOTS])
        aT = sb("aT", [P, SETS, CAD], F32R)
        gk = sb("gk", [P, 4, P], F32R)
        mpart = sb("mpart", [P, CHUNKS, CT * NH])
        mraw = sb("mraw", [P, CT, NH])
        caT = sb("caT", [P, B, CT, NT])
        rl = sb("rl", [P, CT, NH])
        s2 = sb("s2", [P, CT * NH, NT])
        e2 = sb("e2", [P, CT * NH, NT])
        m2 = sb("m2", [P, CT * NH])
        l2 = sb("l2", [P, CT * NH])
        r2 = sb("r2", [P, CT * NH])
        p2 = sb("p2", [P, CT, NH * NT])
        p2x = sb("p2x", [P, TILES, NH, NT])

        with nc.sbuf_tensor("ex", [P, TILES, NH, NK], F32) as ex:
            pass
        with (nc.sbuf_tensor("wq_in", [P, KT, H], F32) as wq_in, nc.sbuf_tensor("wkv_in", [P, 4, CT, H], F32) as wkv_in,
              nc.sbuf_tensor("ctx_tok", [P, B, CAD], F32) as ctx_tok, nc.sbuf_tensor("ctxT", [P, CT, B, P], F32) as ctxT,
              nc.sbuf_tensor("ones_row", [1, P], F32) as ones_row, nc.sbuf_tensor("wqca_in", [NT, H], F32) as wqca_in):
            pass
        with nc.sbuf_tensor("raws", [P, B, KT * SETS, R, P], F32) as raws:
            raw, raw_next = raws[:, 0], raws[:, 1]
        reserve_ex = sb("reserve_ex", [P, TILES * NH * NK])
        with nc.sbuf_tensor("hs1", [P, CT, NH, D], F32) as hs1:
            pass
        xT_hi = sb("xT_hi", [P, 2, KT, P], F32R)
        xT_lo = sb("xT_lo", [P, 2, KT, P], F32R)
        with nc.sbuf_tensor("kT", [P, NH, B, P], F32) as kT, nc.sbuf_tensor("vT_next", [D, NH, P], F32) as vT_next:
            pass
        with nc.sbuf_tensor("gT", [P, SETS, S], F32R) as gT:
            with nc.sbuf_tensor("aTm", [P, R, CAD], F32R) as aTm:
                pass
            with nc.sbuf_tensor("e", [P, ES, CAD], F32) as e:
                pass
        with nc.sbuf_tensor("ns0", [D + 1, R, CAD], F32) as ns0, nc.sbuf_tensor("ns1", [D + 1, R, CAD], F32) as ns1:
            pass
        with nc.sbuf_tensor("hs1T", [P, CT, KT, P], F32) as hs1T:
            pass
        probs = sb("probs", [P, 2, NH, P])
        pT_hi = sb("pT_hi", [P, 2, NH, P], F32R)
        pT_lo = sb("pT_lo", [P, 2, NH, P], F32R)
        res = sb("res", [P, 2, H])

        PS = ctx.enter_context(nc.psum_tensor("PS", [P, 8, BANK], F32))

        def flat(first, banks=2):
            return PS[:, first:first + banks, :].rearrange("p b n -> p (b n)")

        def scores_of(u):
            return PS[:, 4 + 2 * u:6 + 2 * u, :]

        def g_of(u):
            return scores_of(u)[:, :, SW:SW + R * NT].rearrange("p s (r t) -> p s r t", r=R)

        assert ES * CAD + 4 * R * (D + 1) <= 14 * HALF

        def e_half(half):
            return half[:, 0:ES * CAD].rearrange("p (r n) -> p r n", r=ES)

        def xb_half(half):
            return half[:, ES * CAD:ES * CAD + 4 * R * (D + 1)].rearrange("p (k n) -> p k n", k=4)

        def mm(half):
            return half[:, :].rearrange("p (k s n) -> p k s n", k=KT, s=SETS)

        def vw(half):
            return half[:, :].rearrange("p (h f n) -> p h f n", h=NH, f=2)

        def raw_ps_of(n, half):
            return PS[:, 2 * (n % 4) + half, :].rearrange("p (r b k) -> p b r k", r=R // 2, b=B)

        def raw_to(n, half):
            return raws[:, :, n, half * R // 2:(half + 1) * R // 2, :]

        def nsum_of(h):
            return (ns0, ns1)[h // R][:, h % R, :]

        def p2x_bank(i):
            return 2 if i < 2 else 5

        def vw_bank(n):
            return (4 if VW_ORDER.index(n) < 2 else 6) + n % 2

        raw_kept = nc.dram_tensor("raw_kept", (P, KT * SETS, R, P), F32, kind="Internal").ap()
        vT_kept = nc.dram_tensor("vT_kept", (D, NH, P), F32, kind="Internal").ap()

        sel_made, mask_made, gs_set = sem("sel_made"), sem("mask_made"), sem("gs_set")
        ident0, ident_made = sem("ident0"), sem("ident_made")
        wca_ps, wca_made = sem("wca_ps"), sem("wca_made")
        ctx_in_s, wkv_in_s, wq_in_s, wout_in_s = sem("ctx_loaded"), [sem("wk_loaded"), sem("wv_loaded")], [sem("wq_loaded0"), sem("wq_loaded1")], sem("wout_loaded")
        caT_made = sem("caT_made")
        ctxT_ps, ctxT_made, as_hi, as_made = sem("ctxT_ps"), sem("ctxT_made"), sem("as_hi"), sem("as_made")
        wqT_ps, wqT_made = sem("wqT_ps"), sem("wqT_made")
        kv_ps, kv_made = sem("kv_ps"), sem("kv_made")
        raw_ps, raw_made_a, raw_made_d = sem("raw_ps"), sem("raw_made_a"), sem("raw_made_d")
        mmh_made, mml_made, mmg_hi, mmg_made, wk2_made = sem("mmh_made"), sem("mml_made"), sem("mmg_hi"), sem("mmg_made"), sem("wk2_made")
        x_in = [sem("x_in0"), sem("x_in1")]
        xT_ps, xTh_made, xTl_made = sem("xT_ps"), sem("xTh_made"), sem("xTl_made")
        sc_ps, top_made, negmax_made, exp_made = sem("sc_ps"), sem("top_made"), sem("negmax_made"), sem("exp_made")
        gs_hi, gs_made, gT_ps, gT_made = sem("gs_hi"), sem("gs_made"), sem("gT_ps"), sem("gT_made")
        rinv_made = sem("rinv_made")
        vw_ps, vwh_made, vwl_made = sem("vw_ps"), sem("vwh_made"), sem("vwl_made")
        aT_ps, aT_made = sem("aT_ps"), sem("aT_made")
        mx_ps, mx_made, asm_hi, asm_made = sem("mx_ps"), sem("mx_made"), sem("asm_hi"), sem("asm_made")
        xb_in = [sem(f"xb_in{k}") for k in range(4)]
        xh_made, xl_made, ehi_made, elo_made, elo3_made = (sem("xh_made"), sem("xl_made"), sem("ehi_made"), sem("elo_made"),
                                                           sem("elo3_made"))
        rows_zero = sem("rows_zero")
        kept, reload_in, aTm_zero, aTm_ps, aTm_made = (sem("kept"), sem("reload_in"), sem("aTm_zero"), sem("aTm_ps"),
                                                       sem("aTm_made"))
        mpart_made = sem("mpart_made")
        nsa_made, nsd_made = sem("nsa_made"), sem("nsd_made")
        gk_made, sT_ps, e_made, pv_done, eh3_made = sem("gk_made"), sem("sT_ps"), sem("e_made"), sem("pv_done"), sem("eh3_made")
        nT_ps, rl_made, hs1_made, hT_ps, hT_made = sem("nT_ps"), sem("rl_made"), sem("hs1_made"), sem("hT_ps"), sem("hT_made")
        s2_ps, m2_made, s2_made, e2_made = sem("s2_ps"), sem("m2_made"), sem("s2_made"), sem("e2_made")
        l2_made, r2_made, p2_made, p2x_ps, p2x_made = sem("l2_made"), sem("r2_made"), sem("p2_made"), sem("p2x_ps"), sem("p2x_made")
        probs_made, pT_ps, pTh_made, pTl_made = sem("probs_made"), sem("pT_ps"), sem("pTh_made"), sem("pTl_made")
        out_ps, res_made = sem("out_ps"), sem("res_made")
        stored = [sem("stored0"), sem("stored1")]

        block = ctx.enter_context(nc.Block())
        x_rows = x.rearrange("b s n -> (b s) n")
        out_rows = out.rearrange("b s n -> (b s) n")

        @block.sync
        def _(sp):
            sp.dma_start(wqca_in[:, :], wqca).then_inc(stored[0], 16)
            for f in range(2):
                sp.dma_start(wq_in[:, :, f * HALF:(f + 1) * HALF], wq[:, f * HALF:(f + 1) * HALF].rearrange("(j p) n -> p j n", p=P))\
                    .then_inc(wq_in_s[f], 16)
            sp.dma_start(ctx_tok[:, :, :], ctx_in.rearrange("b t n -> t b n")).then_inc(ctx_in_s, 16)
            for w, ready in ((wk, 0), (wkca, 1), (wv, 2), (wvca, 3)):
                sp.dma_start(wkv_in[:, ready], w.rearrange("(c p) n -> p c n", p=P)).then_inc(wkv_in_s[ready // 2], 16)
            sp.wait_ge(mask_made, 3)
            sp.wait_ge(rows_zero, 3)
            sp.dma_start(vT[D:D + 1, 0, :], ones_row[:, :]).then_inc(stored[1], 16)
            sp.wait_ge(kv_made, 2 * NH)
            sp.dma_start(vT_kept, vT_next[:, :, :]).then_inc(reload_in, 16)

            def load_x(b, i, u):
                sp.dma_start(xin[:, u, :], x_rows[bass.ds(i * P + b * S, P), :]).then_inc(x_in[u], 16)
            load_x(0, 0, 0)
            load_x(0, 1, 1)
            for j in range(KT):
                sp.wait_ge(raw_made_a, (j + 1) * SETS)
                sp.wait_ge(raw_made_d, (j + 1) * SETS)
                sp.dma_start(raw_kept[:, j * SETS:(j + 1) * SETS], raw_next[:, j * SETS:(j + 1) * SETS]).then_inc(kept, 16)
            sp.dma_start(wh[0:D, :, :], wout.rearrange("(h d) n -> d h n", d=D)).then_inc(wout_in_s, 16)
            sp.dma_start(wh[D:D + 1, 0, :], bout.rearrange("(a n) -> a n", a=1)).then_inc(wout_in_s, 16)
            for b in range(B):
                with sp.Fori(1, TILES // 2) as ni:
                    i = ni * 2
                    for u in range(2):
                        sp.wait_ge(xT_ps, i + (b * TILES + u - 1))
                        load_x(b, i + u, u)
                for s in range(SETS):
                    def load_xb(kt, k):
                        sp.dma_start(xb[:, k, :, 0:D], x_rows[bass.ds(kt * P + b * S, P), s * R * D:(s + 1) * R * D]
                                     .rearrange("p (r d) -> p r d", r=R)).then_inc(xb_in[k], 16)
                    for k in range(4):
                        if b or s:
                            sp.wait_ge(xl_made, b * 2 * TILES + s * TILES + k - 3)
                        load_xb(k, k)
                    with sp.Fori(1, TILES // 4) as nkt:
                        kt = nkt * 4
                        for k in range(4):
                            sp.wait_ge(xl_made, kt + (b * 2 * TILES + s * TILES + k - 3))
                            load_xb(kt + k, k)
                sp.wait_ge(xT_ps, (b + 1) * TILES)
                load_x(b, 0, 0)
                load_x(b, 1, 1)
                if b + 1 < B:
                    sp.wait_ge(vw_ps, (b + 1) * 2 * NH)
                    sp.dma_start(vT[0:D], vT_kept).then_inc(reload_in, 16)

                def store(i, u):
                    sp.wait_ge(res_made, i + (b * TILES + 2))
                    sp.dma_start(out_rows[bass.ds(i * P + b * S, P), :], res[:, u, :]).then_inc(stored[u], 16)

                def store_and_load(steps):
                    with steps as ni:
                        i = ni * 2
                        for u in range(2):
                            store(i + u, u)
                            load_x(b, i + (u + 2), u)
                store_and_load(sp.Fori(0, RAW_AT // 2))
                if b + 1 < B:
                    sp.wait_ge(kept, KT * 16)
                    sp.wait_ge(probs_made, b * TILES + RAW_AT)
                    for j in range(KT):
                        sp.dma_start(raw[:, j * SETS:(j + 1) * SETS], raw_kept[:, j * SETS:(j + 1) * SETS]).then_inc(reload_in, 16)
                store_and_load(sp.Fori(RAW_AT // 2, TILES // 2 - 1))
                for u in range(2):
                    store(TILES - 2 + u, u)
                    if b + 1 < B:
                        load_x(b + 1, u, u)
            for u in range(2):
                sp.wait_ge(stored[u], 16 + B * TILES // 2 * 16)
            sp.wait_ge(kept, KT * 16)

        @block.gpsimd
        def _(pool):
            nc.gpsimd.memset(one[:, :], 1.0).then_inc(ident0, 1)
            nc.gpsimd.memset(ident[:, :], 0.0).then_inc(ident0, 1)
            nc.gpsimd.memset(headmask[:, :, :], 1.0).then_inc(ident0, 1)
            pool.wait_ge(ident0, 3)
            nc.gpsimd.affine_select(out=ident[:, :], in_=ident[:, :], compare_op=ALU.not_equal, fill=1.0, base=0,
                                    pattern=[[-1, P]], channel_multiplier=1).then_inc(ident_made, 1)
            nc.gpsimd.affine_select(out=headmask[:, :, :], in_=headmask[:, :, :], compare_op=ALU.is_ge, fill=0.0, base=0,
                                    pattern=[[P, KT], [-D, NH]], channel_multiplier=1).then_inc(ident0, 1)
            pool.wait_ge(ident0, 4)
            nc.gpsimd.affine_select(out=headmask[:, :, :], in_=headmask[:, :, :], compare_op=ALU.is_gt, fill=0.0, base=D,
                                    pattern=[[-P, KT], [D, NH]], channel_multiplier=-1).then_inc(mask_made, 1)
            nc.gpsimd.memset(ones_row[:, :], 1.0).then_inc(mask_made, 1)
            pool.wait_ge(mask_made, 2)
            nc.gpsimd.memset(ones_row[:, NK:P], 0.0).then_inc(mask_made, 1)
            nc.gpsimd.memset(sel[:, :, :], 1.0).then_inc(sel_made, 1)
            pool.wait_ge(sel_made, 1)
            for n, (i, c) in enumerate(pairs):
                base = (CAD - 1) * P * i - (S - 1) * P * c
                nc.gpsimd.affine_select(out=sel[:, n, :], in_=sel[:, n, :], compare_op=ALU.is_ge, fill=0.0, base=base,
                                        pattern=[[CAD - 1, P]], channel_multiplier=-(S - 1)).then_inc(sel_made, 1)
            pool.wait_ge(sel_made, 1 + len(pairs))
            for n, (i, c) in enumerate(pairs):
                base = (CAD - 1) * P * i - (S - 1) * P * c
                nc.gpsimd.affine_select(out=sel[:, n, :], in_=sel[:, n, :], compare_op=ALU.is_gt, fill=0.0,
                                        base=(S - 1) - base, pattern=[[-(CAD - 1), P]],
                                        channel_multiplier=S - 1).then_inc(sel_made, 1)
            with pool.Fori(0, B) as b:
                def key_stack(s, kt, k):
                    nc.gpsimd.tensor_tensor(gk[:, k, :], gT[:, s, bass.ds(kt * P, P)].bitcast(F32),
                                            one[:, 0:1].broadcast_to([P, P]), ALU.mult).then_inc(gk_made, 1)

                def x_low(kt, k):
                    pool.wait_ge(xh_made, b * 2 * TILES + kt + 1)
                    nc.gpsimd.tensor_tensor(xb_half(mm_lo)[:, k, :], xb[:, k].rearrange("p r d -> p (r d)"),
                                            xb_half(mm_hi)[:, k, :].bitcast(F32), ALU.subtract).then_inc(xl_made, 1)

                def low3(kt, k):
                    at3 = k % 2 * R + R - 1
                    pool.wait_ge(eh3_made, b * 2 * TILES + kt + 1)
                    nc.gpsimd.tensor_tensor(e_half(mm_lo)[:, at3, :], e[:, at3, :], e_half(mm_hi)[:, at3, :].bitcast(F32),
                                            ALU.subtract).then_inc(elo3_made, 1)

                pool.wait_ge(wca_made, 1)
                pool.wait_ge(res_made, 1 + b * TILES)
                for s in range(SETS):
                    nc.gpsimd.tensor_tensor(mm(mm_hi)[:, :, s, SW:BANK].rearrange("p k (r t) -> p k r t", r=R), wca[:, :, s * R:(s + 1) * R, :],
                                            one[:, 0:1].unsqueeze(2).unsqueeze(3).broadcast_to([P, KT, R, NT]), ALU.mult).then_inc(mmg_hi, 1)
                pool.wait_ge(mmg_hi, b * SETS + SETS)
                for s in range(SETS):
                    nc.gpsimd.tensor_tensor(mm(mm_lo)[:, :, s, SW:BANK].rearrange("p k (r t) -> p k r t", r=R), wca[:, :, s * R:(s + 1) * R, :],
                                            mm(mm_hi)[:, :, s, SW:BANK].bitcast(F32).rearrange("p k (r t) -> p k r t", r=R), ALU.subtract)\
                        .then_inc(mmg_made, 1)

                pool.wait_ge(gT_made, (b + 1) * TILES)
                key_stack(0, 0, 0)
                key_stack(0, 1, 1)
                key_stack(0, 2, 2)
                x_low(0, 0)
                for s in range(SETS):
                    at = s * TILES

                    def step(kt, k, first=False, last=False):
                        if not (first and s == 0 and k == 0):
                            pool.wait_ge(sT_ps, b * 128 + at * 4 + kt * 4 + 4 * k)
                        if last and k >= 1:
                            if s + 1 < SETS:
                                key_stack(s + 1, k - 1, k - 1)
                        else:
                            key_stack(s, kt + (k + 3), (k + 3) % 4)
                        if not (last and k == 3 and s + 1 == SETS):
                            x_low(kt + (at + k + 1), (k + 1) % 4)
                        low3(kt + (at + k), k)
                    for k in range(4):
                        step(0, k, first=True)
                    with pool.Fori(1, TILES // 4 - 1) as nkt:
                        kt = nkt * 4
                        for k in range(4):
                            step(kt, k)
                    for k in range(4):
                        step(TILES - 4, k, last=True)
                pool.wait_ge(rinv_made, (b + 1) * TILES)
                pool.wait_ge(s2_ps, b + 1)
                def normalise(i, u, p2x_part=None):
                    nc.gpsimd.tensor_tensor(probs[:, u, :, 0:NK], ex[:, bass.ds(i, 1)].rearrange("p a h k -> p (a h) k"),
                                            rinv[:, bass.ds(i, 1), :].rearrange("p a h -> p (a h)").unsqueeze(2)
                                            .broadcast_to([P, NH, NK]), ALU.mult)
                    if p2x_part is not None:
                        pool.wait_ge(p2x_made, 2 * b + p2x_part)
                    nc.gpsimd.tensor_tensor(probs[:, u, :, NK:P], p2x[:, bass.ds(i, 1)].rearrange("p a h k -> p (a h) k"),
                                            one[:, 0:1].unsqueeze(2).broadcast_to([P, NH, NT]), ALU.mult).then_inc(probs_made, 1)
                normalise(0, 0, 1)
                normalise(1, 1, 2)
                with pool.Fori(1, TILES // 2) as ni:
                    i = ni * 2
                    for u in range(2):
                        pool.wait_ge(pT_ps, b * TILES + i + (u - 1))
                        normalise(i + u, u)

        @block.scalar
        def _(act):
            act.wait_ge(rows_zero, 1)
            for h in range(NH):
                act.wait_ge(wqT_ps, h + 1)
                nc.scalar.activation(wh[0:D, h, :], flat(2 * (h % 2))[0:D, 0:H], ACT.Copy).then_inc(wqT_made, 1)
            for n in range(KT * SETS):
                act.wait_ge(raw_ps, n + 1)
                nc.scalar.activation(raw_to(n, 0), raw_ps_of(n, 0), ACT.Copy).then_inc(raw_made_a, 1)
            with act.Fori(0, B) as b:
                def xT(i, u, ring=True):
                    act.wait_ge(xT_ps, b * TILES + i + 1)
                    if ring:
                        act.wait_ge(sc_ps, b * TILES + i + (-1))
                    nc.scalar.activation(xT_hi[:, u].rearrange("p k n -> p (k n)"), flat(0)[:, 0:H],
                                         ACT.Copy).then_inc(xTh_made, 1)
                xT(0, 0, False)

                act.wait_ge(raw_made_a, KT * SETS)
                act.wait_ge(raw_made_d, KT * SETS)
                act.wait_ge(reload_in, 16 + b * RELOADS)
                act.wait_ge(res_made, 1 + b * TILES)

                def mm_high(n):
                    nc.scalar.activation(mm(mm_hi)[:, n // 2, n % 2, 0:SW].rearrange("p (r k) -> p r k", r=R),
                                         raw[:, n, :, 0:NK], ACT.Copy).then_inc(mmh_made, 1)

                def soft(i, u):
                    act.wait_ge(negmax_made, b * TILES + i + 1)
                    for h in range(NH):
                        last = nc.scalar.activation(
                            ex[:, bass.ds(i, 1), h, :].rearrange("p a k -> p (a k)"),
                            scores_of(u)[:, h // R, (h % R) * NK:(h % R + 1) * NK], ACT.Exp,
                            bias=negmax[:, u, h:h + 1], scale=SCALE, accum_out=sums[:, u, h:h + 1])
                    last.then_inc(exp_made, 1)

                def g(i):
                    act.wait_ge(gT_ps, b * TILES + i + 1)
                    nc.scalar.activation(gT[:, :, bass.ds(i * P, P)], PS[:, 1, P:P + SETS * P].rearrange("p (s n) -> p s n", s=SETS),
                                         ACT.Copy).then_inc(gT_made, 1)

                mm_high(0)
                mm_high(1)
                for n in range(2, KT * SETS):
                    mm_high(n)
                xT(1, 1, False)
                act.wait_ge(aTm_ps, b + 1)
                act.wait_ge(aTm_zero, b + 1)
                for r in range(R):
                    nc.scalar.activation(aTm[r * SLOTS:r * SLOTS + 16, r, :], PS[r * SLOTS:r * SLOTS + 16, 2, 0:CAD],
                                         ACT.Copy).then_inc(aTm_made, 1)

                act.wait_ge(kept, KT * 16)
                xT(2, 0)
                soft(0, 0)
                g(0)
                xT(3, 1)
                soft(1, 1)
                g(1)
                with act.Fori(1, TILES // 2 - 1) as ni:
                    i = ni * 2
                    for u in range(2):
                        xT(i + (u + 2), u)
                        soft(i + u, u)
                        g(i + u)
                soft(TILES - 2, 0)
                g(TILES - 2)

                def vw_high(*ns):
                    for n in ns:
                        act.wait_ge(vw_ps, b * 2 * NH + VW_ORDER.index(n) + 1)
                        nc.scalar.activation(vw(mm_hi)[:, n // 2, n % 2, :], PS[:, vw_bank(n), 0:HALF], ACT.Copy).then_inc(vwh_made, 1)
                vw_high(14, 15)
                g(TILES - 1)
                soft(TILES - 1, 1)

                def x_high(kt, k):
                    act.wait_ge(xb_in[k], b * 128 + (kt - k) * 4 + 16)
                    nc.scalar.activation(xb_half(mm_hi)[:, k, :], xb[:, k].rearrange("p r d -> p (r d)"), ACT.Copy)\
                        .then_inc(xh_made, 1)

                x_high(0, 0)
                act.wait_ge(aT_ps, b * SETS + 1)
                nc.scalar.activation(aT[:, 0, :], PS[:, 0, 0:CAD], ACT.Copy).then_inc(aT_made, 1)

                def take_sums(s, r):
                    act.wait_ge(pv_done, b * 128 + s * 64 + (61 + r))
                    nc.scalar.activation(nsum_of(s * R + r), PS[0:D + 1, r, 0:CAD], ACT.Copy).then_inc(nsa_made, 1)

                def key_exps(kt, k, next_x=True, sums_of=None):
                    for r in range(R):
                        act.wait_ge(sT_ps, b * 128 + kt * 4 + (r + 1))
                        nc.scalar.activation(e[:, k % 2 * R + r, :], PS[:, 4 + r, 0:CAD], ACT.Exp, scale=SCALE).then_inc(e_made, 1)
                        if r == 1 and next_x:
                            x_high(kt + 1, (k + 1) % 4)
                        if sums_of is not None and r == (2, 0)[k]:
                            take_sums(sums_of, (0, 2)[k])
                    nc.scalar.activation(e_half(mm_hi)[:, k % 2 * R + R - 1, :], PS[:, 3 + R, 0:CAD], ACT.Exp, scale=SCALE)\
                        .then_inc(eh3_made, 1)
                for u in range(2):
                    act.wait_ge(stored[u], b * TILES // 2 * 16 + 16)
                for s in range(SETS):
                    at = s * TILES
                    for k in range(4):
                        key_exps(at + k, k, sums_of=(0 if s and k < 2 else None))
                    with act.Fori(1, TILES // 4 - 1) as nkt:
                        kt = nkt * 4
                        for k in range(4):
                            key_exps(kt + (at + k), k)
                    for k in range(4):
                        key_exps(at + TILES - 4 + k, k, next_x=(k < 3 or s + 1 < SETS))
                for r in (0, 2):
                    take_sums(1, r)

                def hT(c):
                    act.wait_ge(hT_ps, b * CT + c + 1)
                    nc.scalar.activation(hs1T[:, c].rearrange("p k n -> p (k n)"), flat((4, 2, 4)[c])[:, 0:H],
                                         ACT.Copy).then_inc(hT_made, 1)
                vw_high(0, 1, 2, 3)
                hT(0)
                vw_high(4, 5)
                hT(1)
                vw_high(6, 7)
                hT(2)
                vw_high(8, 9)
                act.wait_ge(s2_made, b + 1)
                nc.scalar.activation(e2[:, :, :], s2[:, :, :], ACT.Exp, scale=SCALE).then_inc(e2_made, 1)
                vw_high(10, 11)

                def pT(i, u, ring=True):
                    act.wait_ge(pT_ps, b * TILES + i + 1)
                    if ring:
                        act.wait_ge(out_ps, b * TILES + i + (-1))
                    nc.scalar.activation(pT_hi[:, u].rearrange("p h n -> p (h n)"), flat(2 * u), ACT.Copy).then_inc(pTh_made, 1)
                pT(0, 0, False)
                vw_high(12, 13)
                pT(1, 1, False)
                with act.Fori(1, TILES // 2) as ni:
                    i = ni * 2
                    for u in range(2):
                        pT(i + u, u)

        @block.vector
        def _(dve):
            nc.vector.memset(gs[:, :, :, :], 0.0).then_inc(gs_set, 1)
            nc.vector.memset(wh[64:P], 0.0).then_inc(rows_zero, 1)
            dve.wait_ge(wca_ps, 1)
            dve.wait_ge(mask_made, 3)
            for j in range(KT):
                last = nc.vector.tensor_tensor(wca[:, j], PS[:, 0, j * NT:(j + 1) * NT].unsqueeze(1).broadcast_to([P, NH, NT]),
                                               headmask[:, j, :].unsqueeze(2).broadcast_to([P, NH, NT]), ALU.mult)
            last.then_inc(wca_made, 1)
            for rows in (kT, vT):
                nc.vector.memset(rows[64:P], 0.0).then_inc(rows_zero, 1)
            nc.vector.memset(as_[:, :, :, :], 0.0).then_inc(gs_set, 1)
            nc.vector.memset(xb[:, :, :, :], 1.0).then_inc(gs_set, 1)
            nc.vector.memset(res[:, :, :], 0.0).then_inc(res_made, 1)
            nc.vector.memset(mpart[:, :, :], 0.0).then_inc(mx_made, 1)
            nc.vector.memset(mraw[:, :, :], 0.0).then_inc(mx_made, 1)
            dve.wait_ge(gs_set, 1)
            nc.vector.memset(gs[:, :, :, 16:18], 1.0).then_inc(gs_set, 1)
            dve.wait_ge(ctxT_ps, 1)
            nc.vector.tensor_copy(ctxT[:, :, :, :].rearrange("p c b n -> p (c b n)"), flat(4)[:, 0:B * CAD]).then_inc(ctxT_made, 1)
            dve.wait_ge(ctxT_made, 1)
            nc.vector.tensor_copy(caT[:, :, :, :], ctxT[:, :, :, NK:P].rearrange("p c b t -> p b c t")).then_inc(caT_made, 1)
            for h in range(NH):
                dve.wait_ge(kv_ps, h + 1)
                nc.vector.tensor_copy(kT[0:D, h].rearrange("p b n -> p (b n)"), PS[0:D, 4 + h % 4, 0:B * P])
                for b, to in enumerate((vT, vT_next)):
                    nc.vector.tensor_copy(to[0:D, h], PS[0:D, 4 + h % 4, (B + b) * P:(B + b + 1) * P]).then_inc(kv_made, 1)
            for n in range(KT * SETS):
                dve.wait_ge(raw_ps, n + 1)
                nc.vector.tensor_copy(raw_to(n, 1), raw_ps_of(n, 1)).then_inc(raw_made_d, 1)
            with dve.Fori(0, B) as b:
                def xT(i, u):
                    dve.wait_ge(xTh_made, b * TILES + i + 1)
                    nc.vector.tensor_tensor(xT_lo[:, u].rearrange("p k n -> p (k n)"), flat(0)[:, 0:H],
                                            xT_hi[:, u].bitcast(F32).rearrange("p k n -> p (k n)"), ALU.subtract).then_inc(xTl_made, 1)

                xT(0, 0)
                def mm_low(n):
                    dve.wait_ge(mmh_made, b * KT * SETS + n + 1)
                    nc.vector.tensor_tensor(mm(mm_lo)[:, n // 2, n % 2, 0:SW].rearrange("p (r k) -> p r k", r=R), raw[:, n, :, 0:NK],
                                            mm(mm_hi)[:, n // 2, n % 2, 0:SW].bitcast(F32).rearrange("p (r k) -> p r k", r=R),
                                            ALU.subtract).then_inc(mml_made, 1)

                def gs_half(u, s, lo):
                    return gs[:, u, s * R:(s + 1) * R, 8 * lo:8 * lo + 8].rearrange("p r (a t) -> p r a t", a=2)

                def g_rep(u, s):
                    return g_of(u)[:, s].unsqueeze(2).broadcast_to([P, R, 2, NT])

                def soft(i, u, first=False, between=None):
                    dve.wait_ge(sc_ps, b * TILES + i + 1)
                    def maxima():
                        if not first:
                            dve.wait_ge(exp_made, b * TILES + i + (-1))
                        nc.vector.tensor_reduce(top[:, u, :].rearrange("p (s r) -> p s r", s=SETS), scores_of(u)[:, :, 0:SW].rearrange("p s (r k) -> p s r k", r=R),
                                                AX.X, ALU.max).then_inc(top_made, 1)
                    if between is None:
                        maxima()
                    if not first:
                        dve.wait_ge(gT_ps, b * TILES + i + (-1))
                    for s in range(SETS):
                        nc.vector.tensor_copy(gs_half(u, s, 0).bitcast(F32R), g_rep(u, s)).then_inc(gs_hi, 1)
                    dve.wait_ge(gs_hi, b * 2 * TILES + i * 2 + 2)
                    for s in range(SETS):
                        last = nc.vector.tensor_tensor(gs_half(u, s, 1).bitcast(F32R), g_rep(u, s), gs_half(u, s, 0), ALU.subtract)
                    last.then_inc(gs_made, 1)
                    if between is not None:
                        between()
                        maxima()
                    dve.wait_ge(top_made, b * TILES + i + 1)
                    dve.wait_ge(gs_made, b * TILES + i + 1)
                    nc.vector.tensor_scalar(negmax[:, u, :], top[:, u, :], -SCALE, None, ALU.mult).then_inc(negmax_made, 1)

                def inv(i, u):
                    dve.wait_ge(exp_made, b * TILES + i + 1)
                    nc.vector.reciprocal(rinv[:, bass.ds(i, 1), :].rearrange("p a h -> p (a h)"), sums[:, u, :]).then_inc(rinv_made, 1)

                def units(chunk, ps, banks=2):
                    for p in ps:
                        dve.wait_ge(mx_ps, b * MXB + chunk * UNITS + p + 1)
                        nc.vector.tensor_reduce(mpart[:, bass.ds(chunk, 1), 2 * p:2 * p + 2].rearrange("p a n -> p (a n)"),
                                                PS[:, 2 + p % banks, :].rearrange("p (h n) -> p h n", h=2), AX.X, ALU.max)\
                            .then_inc(mx_made, 1)

                dve.wait_ge(mx_made, 2)
                mm_low(0)
                mm_low(1)
                for n in range(2, KT * SETS):
                    mm_low(n)
                xT(1, 1)
                nc.vector.tensor_copy(wk2[:, :, :, :].rearrange("p k h t -> p (k h) t"),
                                      raw[:, :, :, NK:P].rearrange("p n r t -> p (n r) t")).then_inc(wk2_made, 1)
                nc.vector.memset(aTm[:, :, :].bitcast(F32), 0.0).then_inc(aTm_zero, 1)
                dve.wait_ge(caT_made, 1)
                dve.wait_ge(gs_set, 4)

                def as_half(c, lo):
                    return as_[:, c, :, 0:16].rearrange("p h (a l t) -> p h a l t", a=2, l=2)[:, :, :, lo, :]

                def ca(c):
                    return caT[:, bass.ds(b, 1), c, :].rearrange("p a t -> p (a t)").unsqueeze(1).unsqueeze(1)\
                        .broadcast_to([P, NH, 2, NT])
                for c in range(CT):
                    nc.vector.tensor_copy(as_half(c, 0).bitcast(F32R), ca(c)).then_inc(as_hi, 1)
                dve.wait_ge(as_hi, (b + 1) * CT)
                for c in range(CT):
                    nc.vector.tensor_tensor(as_half(c, 1).bitcast(F32R), ca(c), as_half(c, 0), ALU.subtract).then_inc(as_made, 1)
                xT(2, 0)
                soft(0, 0, True)
                inv(0, 0)
                xT(3, 1)
                soft(1, 1, True)
                inv(1, 1)
                with dve.Fori(1, TILES // 2 - 1) as ni:
                    i = ni * 2 + 1
                    for u in range(2):
                        xT(i + (u + 1), u)
                        soft(i + (u - 1), u)
                        units(ni + (-1), HALVES[u])
                        inv(i + (u - 1), u)
                soft(TILES - 2, 0)
                units(CHUNKS - 2, range(UNITS))
                inv(TILES - 2, 0)
                def vw_low(*ns):
                    for n in ns:
                        dve.wait_ge(vwh_made, b * 2 * NH + VW_ORDER.index(n) + 1)
                        nc.vector.tensor_tensor(vw(mm_lo)[:, n // 2, n % 2, :], PS[:, vw_bank(n), 0:HALF],
                                                vw(mm_hi)[:, n // 2, n % 2, :].bitcast(F32), ALU.subtract).then_inc(vwl_made, 1)

                soft(TILES - 1, 1, between=lambda: vw_low(14, 15))
                units(CHUNKS - 1, range(UNITS), 4)
                inv(TILES - 1, 1)
                dve.wait_ge(mx_made, (b + 1) * MXB + 2)
                nc.vector.tensor_reduce(mraw[:, :, :].rearrange("p c h -> p (c h)"), mpart[:, :, :].rearrange("p k n -> p n k"),
                                        AX.X, ALU.max).then_inc(mpart_made, 1)
                dve.wait_ge(mpart_made, b + 1)
                nc.vector.tensor_scalar(as_[:, :, :, 16].bitcast(F32R), mraw[:, :, :], -1.0, None, ALU.mult).then_inc(asm_hi, 1)
                dve.wait_ge(asm_hi, b + 1)
                nc.vector.scalar_tensor_tensor(as_[:, :, :, 17].bitcast(F32R), mraw[:, :, :], -1.0, as_[:, :, :, 16],
                                               ALU.mult, ALU.subtract).then_inc(asm_made, 1)
                dve.wait_ge(aT_ps, b * SETS + SETS)
                nc.vector.tensor_copy(aT[:, 1, :], PS[:, 1, 0:CAD]).then_inc(aT_made, 1)

                def take_sums(s, r):
                    dve.wait_ge(pv_done, b * 128 + s * 64 + (61 + r))
                    nc.vector.tensor_copy(nsum_of(s * R + r), PS[0:D + 1, r, 0:CAD]).then_inc(nsd_made, 1)

                for s in range(SETS):
                    def high(kt, u, r):
                        dve.wait_ge(e_made, b * 128 + s * 64 + kt * 4 + (r + 1))
                        nc.vector.tensor_copy(e_half(mm_hi)[:, u * R + r, :], e[:, u * R + r, :]).then_inc(ehi_made, 1)

                    def low(kt, u, r):
                        dve.wait_ge(ehi_made, b * 96 + s * 48 + kt * 3 + (r + 1))
                        nc.vector.tensor_tensor(e_half(mm_lo)[:, u * R + r, :], e[:, u * R + r, :],
                                                e_half(mm_hi)[:, u * R + r, :].bitcast(F32), ALU.subtract).then_inc(elo_made, 1)

                    def exp_halves(kt, u, sums_of=None):
                        high(kt, u, 0)
                        if sums_of is not None and u == 1:
                            take_sums(sums_of, 3)
                        high(kt, u, 1)
                        low(kt, u, 0)
                        high(kt, u, 2)
                        if sums_of is not None and u == 0:
                            take_sums(sums_of, 1)
                        low(kt, u, 1)
                        low(kt, u, 2)
                    for u in range(2):
                        exp_halves(u, u, 0 if s else None)
                    with dve.Fori(1, TILES // 2) as nkt:
                        kt = nkt * 2
                        for u in range(2):
                            exp_halves(kt + u, u)
                for r in (1, 3):
                    take_sums(1, r)

                def value_rows(c):
                    at = (0, 2, 0)[c]
                    ps = PS[:, at:at + 2, 0:R * (D + 1)].rearrange("p s (r d) -> p s r d", r=R)
                    dve.wait_ge(nT_ps, b * CT + c + 1)
                    nc.vector.reciprocal(rl[:, c, :].rearrange("p (s r) -> p s r", s=SETS), ps[:, :, :, D]).then_inc(rl_made, 1)
                    dve.wait_ge(rl_made, b * CT + c + 1)
                    for s in range(SETS):
                        last = nc.vector.tensor_tensor(hs1[:, c, s * R:(s + 1) * R, :], ps[:, s, :, 0:D],
                                                       rl[:, c, s * R:(s + 1) * R].unsqueeze(2).broadcast_to([P, R, D]), ALU.mult)
                    last.then_inc(hs1_made, 1)
                vw_low(0, 1)
                value_rows(0)
                value_rows(1)
                vw_low(2, 3)
                value_rows(2)
                vw_low(4, 5, 6, 7, 8, 9)
                dve.wait_ge(s2_ps, b + 1)
                sc2 = PS[:, 0, 0:CT * NH * NT].rearrange("p (g t) -> p g t", t=NT)
                nc.vector.tensor_reduce(m2[:, :], sc2, AX.X, ALU.max).then_inc(m2_made, 1)
                dve.wait_ge(m2_made, b + 1)
                nc.vector.tensor_tensor(s2[:, :, :], sc2, m2[:, :].unsqueeze(2).broadcast_to([P, CT * NH, NT]), ALU.subtract).then_inc(s2_made, 1)
                dve.wait_ge(e2_made, b + 1)
                nc.vector.tensor_reduce(l2[:, :], e2[:, :, :], AX.X, ALU.add).then_inc(l2_made, 1)
                dve.wait_ge(l2_made, b + 1)
                nc.vector.reciprocal(r2[:, :], l2[:, :]).then_inc(r2_made, 1)
                dve.wait_ge(r2_made, b + 1)
                nc.vector.tensor_tensor(p2[:, :, :].rearrange("p c (h t) -> p (c h) t", t=NT), e2[:, :, :],
                                        r2[:, :].unsqueeze(2).broadcast_to([P, CT * NH, NT]), ALU.mult).then_inc(p2_made, 1)
                vw_low(10, 11)
                def pT(i, u):
                    dve.wait_ge(pTh_made, b * TILES + i + 1)
                    nc.vector.tensor_tensor(pT_lo[:, u].rearrange("p h n -> p (h n)"), flat(2 * u),
                                            pT_hi[:, u].bitcast(F32).rearrange("p h n -> p (h n)"), ALU.subtract).then_inc(pTl_made, 1)

                def take_p2x(n, i0, i1):
                    dve.wait_ge(p2x_ps, 2 * b + n + 1)
                    nc.vector.tensor_copy(p2x[:, i0:i1].rearrange("p i h t -> p (i h t)"), PS[:, p2x_bank(i0), i0 * 32:i1 * 32])\
                        .then_inc(p2x_made, 1)
                take_p2x(0, 0, 2)

                def add_x(i, u):
                    dve.wait_ge(out_ps, b * TILES + i + 1)
                    dve.wait_ge(x_in[u], b * TILES * 16 + (TILES // 2 + 1) * 16 + (i - u) * 8)
                    dve.wait_ge(stored[u], 16 + b * (TILES // 2) * 16 + (i - u) * 8)
                    nc.vector.tensor_tensor(res[:, u, :].rearrange("p (f n) -> p f n", f=2), PS[:, 4 + 2 * u:6 + 2 * u, 0:HALF],
                                            xin[:, u, :].rearrange("p (f n) -> p f n", f=2), ALU.add).then_inc(res_made, 1)
                pT(0, 0)
                take_p2x(1, 2, TILES)
                vw_low(12, 13)
                with dve.Fori(0, TILES // 2 - 1) as ni:
                    i = ni * 2
                    for u in range(2):
                        pT(i + (u + 1), 1 - u)
                        add_x(i + u, u)
                pT(TILES - 1, 1)
                add_x(TILES - 2, 0)
                add_x(TILES - 1, 1)

        @block.tensor
        def _(pe):
            mul = nc.tensor.matmul
            pe.wait_ge(stored[0], 16)
            pe.wait_ge(ident_made, 1)
            for j in range(KT):
                last = nc.tensor.transpose(PS[:, 0, j * NT:(j + 1) * NT], wqca_in[:, j * P:(j + 1) * P], ident[0:NT, 0:NT])
            last.then_inc(wca_ps, 1)
            pe.wait_ge(wca_made, 1)
            for h in range(NH):
                if h % R == 0:
                    pe.wait_ge(wq_in_s[h // R], 16)
                if h >= 2:
                    pe.wait_ge(wqT_made, h - 1)
                for j in range(KT):
                    last = nc.tensor.transpose(flat(2 * (h % 2))[0:D, j * P:(j + 1) * P], wq_in[:, j, h * D:(h + 1) * D], ident[:, :])
                last.then_inc(wqT_ps, 1)
            pe.wait_ge(ctx_in_s, 16)
            for c in range(CT):
                for b in range(B):
                    last = nc.tensor.transpose(flat(4)[:, (c * B + b) * P:(c * B + b + 1) * P], ctx_tok[:, b, c * P:(c + 1) * P],
                                               ident[:, :])
            last.then_inc(ctxT_ps, 1)
            pe.wait_ge(ctxT_made, 1)
            for h in range(NH):
                if h >= 4:
                    pe.wait_ge(kv_made, 2 * (h - 3))
                for a in range(2):
                    pe.wait_ge(wkv_in_s[a], 32)
                    ps = PS[0:D, 4 + h % 4, a * B * P:(a + 1) * B * P].rearrange("p (b n) -> p b n", b=B)
                    for w, t0, t1 in ((2 * a, 0, NK), (2 * a + 1, NK, P)):
                        for c in range(CT):
                            last = mul(ps[:, :, t0:t1], wkv_in[:, w, c, h * D:(h + 1) * D], ctxT[:, c, :, t0:t1],
                                       start=(c == 0), stop=(c == CT - 1))
                last.then_inc(kv_ps, 1)
            pe.wait_ge(wqT_made, NH)
            for n in range(KT * SETS):
                if n < 2:
                    pe.wait_ge(kv_made, 2 * R * (n + 1))
                if n >= 4:
                    pe.wait_ge(raw_made_a, n - 3)
                    pe.wait_ge(raw_made_d, n - 3)
                for r in range(R):
                    h = (n % 2) * R + r
                    last = mul(flat(2 * (n % 4))[:, r * B * P:(r + 1) * B * P], wh[:, h, (n // 2) * P:(n // 2 + 1) * P],
                               kT[:, h].rearrange("p b n -> p (b n)"), start=True, stop=True)
                last.then_inc(raw_ps, 1)
            pe.wait_ge(stored[1], 16)
            pe.wait_ge(raw_made_a, KT * SETS - 1)
            pe.wait_ge(raw_made_d, KT * SETS - 1)
            with pe.Fori(0, B) as b:
                def xT(i, u, first=False):
                    pe.wait_ge(x_in[u], b * TILES * 16 + (i - u) * 8 + 16)
                    if not first:
                        pe.wait_ge(gT_made, b * TILES + i + (-2))
                    for j in range(KT):
                        last = nc.tensor.transpose(flat(0)[:, j * P:(j + 1) * P], xin[:, u, j * P:(j + 1) * P], ident[:, :])
                    last.then_inc(xT_ps, 1)

                def pair_scores(chunk, p, banks=2):
                    pe.wait_ge(mx_made, b * MXB + chunk * UNITS + max(min(p, 1) + 1, p + 3 - banks))
                    c, h = 2 * p // NH, 2 * p % NH
                    for k in range(2):
                        last = mul(PS[:, 2 + p % banks, k * 2 * P:(k + 1) * 2 * P], aTm[:, (h + k) % R, c * P:(c + 1) * P],
                                   gT[:, h // R, bass.ds(chunk * 2 * P, 2 * P)], start=True, stop=True)
                    last.then_inc(mx_ps, 1)

                def step(i, u, next_x=True, first=False, g=True, g_first=False, chunk=None, pairs=(), spaced=3, begin=False):
                    if next_x:
                        xT(i + 1, 1 - u)
                    pe.wait_ge(xTh_made if begin else xTl_made, b * TILES + i + 1)
                    if not first:
                        pe.wait_ge(exp_made, b * TILES + i + (-1))
                    done = 0
                    todo = list(pairs)
                    at = 31 - spaced * len(todo)
                    for j in range(KT):
                        if begin and j == 3:
                            xT(1, 1, True)
                        for n, (l, rr) in enumerate(((xT_hi, mm_hi), (xT_lo, mm_hi), (xT_hi, mm_lo))):
                            if begin:
                                if n == 0:
                                    pe.wait_ge(mmh_made, b * KT * SETS + (j + 1) * SETS)
                                elif n == 1:
                                    pe.wait_ge(xTl_made, b * TILES + i + 1)
                                else:
                                    pe.wait_ge(mml_made, b * KT * SETS + (j + 1) * SETS)
                                    pe.wait_ge(mmg_made, (b + 1) * SETS)
                            for s in range(SETS):
                                last = mul(scores_of(u)[:, s, :], l[:, u, j, :], mm(rr)[:, j, s, :],
                                           start=(j == 0 and n == 0), stop=(j == KT - 1 and n == 2))
                                done += 1
                                if g and done == 20:
                                    if next_x:
                                        pe.wait_ge(xTl_made, b * TILES + i + 2)
                                    g_stack(i + (-1), 1 - u, first=g_first)
                                if todo and done >= at and (done - at) % spaced == 0:
                                    pair_scores(chunk, todo.pop(0))
                    last.then_inc(sc_ps, 1)
                    assert not todo

                def g_stack(i, u, first=False):
                    if not first:
                        pe.wait_ge(gT_made, b * TILES + i)
                    pe.wait_ge(gs_made, b * TILES + i + 1)
                    for s in range(SETS):
                        last = nc.tensor.transpose(PS[:, 1, P + s * P:P + (s + 1) * P],
                                                   gs[:, u, s * R:(s + 1) * R, :].rearrange("p r n -> p (r n)"), ident[:, :])
                    last.then_inc(gT_ps, 1)

                xT(0, 0, True)
                pe.wait_ge(mmg_hi, (b + 1) * SETS)
                step(0, 0, False, True, False, begin=True)
                pe.wait_ge(xTl_made, b * TILES + 2)
                xT(2, 0, True)
                pe.wait_ge(raw_made_a, KT * SETS)
                pe.wait_ge(raw_made_d, KT * SETS)
                pe.wait_ge(as_made, (b + 1) * CT)
                for c in range(CT):
                    last = nc.tensor.transpose(PS[:, 2, c * P:(c + 1) * P], as_[:, c, 0:R, :].rearrange("p r n -> p (r n)"), ident[:, :])
                last.then_inc(aTm_ps, 1)
                step(1, 1, False, True, g_first=True)
                pe.wait_ge(aTm_made, (b + 1) * R)
                step(2, 0)
                with pe.Fori(1, TILES // 2 - 1) as ni:
                    i = ni * 2 + 1
                    for u in range(2):
                        step(i + u, 1 - u, chunk=ni + (-1), pairs=HALVES[u])
                pe.wait_ge(gT_made, (b + 1) * TILES - 2)
                step(TILES - 1, 1, next_x=False, chunk=CHUNKS - 2, pairs=range(UNITS), spaced=2)
                def vw_product(*ns):
                    for n in ns:
                        h, f = n // 2, n % 2
                        if VW_ORDER.index(n) >= 2:
                            pe.wait_ge(vwl_made, b * 2 * NH + VW_ORDER.index(n) - 1)
                        mul(PS[:, vw_bank(n), 0:HALF], vT[:, h, :], wh[:, h, f * HALF:(f + 1) * HALF],
                            start=True, stop=True).then_inc(vw_ps, 1)
                pe.wait_ge(wout_in_s, 32)
                pe.wait_ge(reload_in, 16 + b * RELOADS)
                pe.wait_ge(exp_made, (b + 1) * TILES - 1)
                vw_product(14, 15)
                g_stack(TILES - 1, 1)

                pe.wait_ge(gT_made, (b + 1) * TILES)
                for p in range(UNITS):
                    if p == 2:
                        pe.wait_ge(vwl_made, b * 2 * NH + 2)
                    pair_scores(CHUNKS - 1, p, 4)
                pe.wait_ge(asm_made, b + 1)
                for s in range(SETS):
                    for c in range(CT):
                        last = nc.tensor.transpose(PS[:, s, c * P:(c + 1) * P],
                                                   as_[:, c, s * R:(s + 1) * R, :].rearrange("p r n -> p (r n)"), ident[:, :])
                    last.then_inc(aT_ps, 1)
                pe.wait_ge(aT_made, (b + 1) * SETS)
                pe.wait_ge(exp_made, (b + 1) * TILES)

                def sT(s, kt, k, r, first=False):
                    if not first:
                        if r < R - 1:
                            pe.wait_ge(e_made, b * 128 + s * 64 + kt * 4 + (r - 3))
                        else:
                            pe.wait_ge(eh3_made, b * 2 * TILES + s * TILES + kt)
                    if r == 0:
                        pe.wait_ge(gk_made, b * 2 * TILES + s * TILES + kt + 1)
                    mul(PS[:, 4 + r, 0:CAD], gk[r * SLOTS:r * SLOTS + 18, k, :], aT[r * SLOTS:r * SLOTS + 18, s, :],
                        start=True, stop=True).then_inc(sT_ps, 1)

                def pv(s, kt, k, r, start=False, stop=False):
                    if r == 0:
                        pe.wait_ge(xl_made, b * 2 * TILES + s * TILES + kt + 1)
                    if r < R - 1:
                        pe.wait_ge(elo_made, b * 96 + s * 48 + kt * 3 + (r + 1))
                    else:
                        pe.wait_ge(elo3_made, b * 2 * TILES + s * TILES + kt + 1)
                    for n, (xx, ee) in enumerate(((mm_hi, mm_hi), (mm_lo, mm_hi), (mm_hi, mm_lo))):
                        last = mul(PS[0:D + 1, r, 0:CAD], xb_half(xx)[:, k, r * (D + 1):(r + 1) * (D + 1)],
                                   e_half(ee)[:, k % 2 * R + r, :], start=(start and n == 0), stop=(stop and n == 2))
                    last.then_inc(pv_done, 1)

                def key_tile(s, kt, k, start=False, left=TILES):
                    for r in range(R):
                        if start and s:
                            if r % 2:
                                pe.wait_ge(nsd_made, b * R + (r + 1) // 2)
                            else:
                                pe.wait_ge(nsa_made, b * R + r // 2 + 1)
                        pv(s, kt, k, r, start, left == 1)
                        dk, rr = (r + AHEAD) // R, (r + AHEAD) % R
                        if dk < left:
                            sT(s, kt + dk, (k + dk) % 4, rr)
                        elif s + 1 < SETS:
                            sT(s + 1, dk - left, (k + dk) % 4, rr)

                for n in range(AHEAD):
                    sT(0, n // R, n // R, n % R, n < R)
                for s in range(SETS):
                    for kt in range(4):
                        key_tile(s, kt, kt, start=(kt == 0))
                    with pe.Fori(1, TILES // 4 - 1) as nkt:
                        kt = nkt * 4
                        for k in range(4):
                            key_tile(s, kt + k, k)
                    for k in range(4):
                        key_tile(s, TILES - 4 + k, k, left=4 - k)

                def sums_T(c):
                    for h in range(NH):
                        at = (h % R) * (D + 1)
                        last = nc.tensor.transpose(PS[:, (0, 2, 0)[c] + h // R, at:at + D + 1], nsum_of(h)[:, c * P:(c + 1) * P],
                                                   ident[0:D + 1, 0:D + 1])
                    last.then_inc(nT_ps, 1)

                def values_T(c):
                    pe.wait_ge(hs1_made, b * CT + c + 1)
                    for j in range(KT):
                        last = nc.tensor.transpose(flat((4, 2, 4)[c])[:, j * P:(j + 1) * P],
                                                   hs1[:, c].rearrange("p h d -> p (h d)")[:, j * P:(j + 1) * P], ident[:, :])
                    last.then_inc(hT_ps, 1)
                vw_product(0, 1)
                pe.wait_ge(nsa_made, (b + 1) * R)
                pe.wait_ge(nsd_made, (b + 1) * R)
                sums_T(0)
                sums_T(1)
                vw_product(2, 3)
                pe.wait_ge(hs1_made, b * CT + 1)
                sums_T(2)
                values_T(0)
                vw_product(4, 5)
                values_T(1)
                vw_product(6, 7)
                pe.wait_ge(hT_made, b * CT + 1)
                values_T(2)
                vw_product(8, 9)
                pe.wait_ge(wk2_made, b + 1)
                for c in range(CT):
                    pe.wait_ge(hT_made, b * CT + c + 1)
                    for j in range(KT):
                        last = mul(PS[:, 0, c * 32:(c + 1) * 32], hs1T[:, c, j, :], wk2[:, j].rearrange("p h t -> p (h t)"),
                                   start=(j == 0), stop=(j == KT - 1))
                last.then_inc(s2_ps, 1)
                vw_product(10, 11)
                def pT(i, u, first=False):
                    pe.wait_ge(probs_made, b * TILES + i + 1)
                    if not first:
                        pe.wait_ge(pTl_made, b * TILES + i + (-1))
                    for h in range(NH):
                        last = nc.tensor.transpose(flat(2 * u)[:, h * P:(h + 1) * P], probs[:, u, h, :], ident[:, :])
                    last.then_inc(pT_ps, 1)

                pe.wait_ge(sel_made, 1 + 2 * len(pairs))
                pe.wait_ge(p2_made, b + 1)
                for n, (i, c) in enumerate(pairs):
                    last = mul(PS[:, p2x_bank(i), i * 32:(i + 1) * 32], sel[:, n, :], p2[:, c, :],
                               start=(n == 0 or pairs[n - 1][0] != i), stop=(n + 1 == len(pairs) or pairs[n + 1][0] != i))
                    if n + 1 == len(pairs) or (i, pairs[n + 1][0]) == (1, 2):
                        last.then_inc(p2x_ps, 1)
                    if (i, pairs[min(n + 1, len(pairs) - 1)][0]) == (4, 5):
                        pT(0, 0, True)

                def output(i, u, first=False):
                    pe.wait_ge(pTl_made, b * TILES + i + 1)
                    if not first:
                        pe.wait_ge(res_made, 1 + b * TILES + i + (-1))
                    for h in range(NH):
                        if first and i == 0:
                            pe.wait_ge(vwl_made, b * 2 * NH + max(VW_ORDER.index(2 * k + 1) + 1 for k in range(h + 1)))
                        for n, (l, rr) in enumerate(((pT_hi, mm_hi), (pT_hi, mm_lo), (pT_lo, mm_hi))):
                            for f in range(2):
                                last = mul(PS[:, 4 + 2 * u + f, 0:HALF], l[:, u, h, :], vw(rr)[:, h, f, :],
                                           start=(h == 0 and n == 0), stop=(h == NH - 1 and n == 2))
                    last.then_inc(out_ps, 1)

                vw_product(12, 13)
                pe.wait_ge(p2x_made, 2 * b + 2)
                pT(1, 1, True)
                output(0, 0, True)
                pT(2, 0)
                output(1, 1, True)
                with pe.Fori(1, TILES // 2 - 1) as ni:
                    i = ni * 2
                    for u in range(2):
                        pT(i + (u + 1), 1 - u)
                        output(i + u, u)
                pT(TILES - 1, 1)
                output(TILES - 2, 0)
                output(TILES - 1, 1)


_INS = ['x', 'ctx_768', 'L0_xattn_Wq', 'L0_xattn_Wk', 'L0_xattn_Wv', 'L0_xattn_Wq_ca', 'L0_xattn_Wk_ca', 'L0_xattn_Wv_ca',
        'L0_xattn_Wout', 'L0_xattn_b_out']


def kernel(**inputs):
    import concourse.bacc as bacc
    from concourse.bass_utils import run_bass_kernel_spmd as run

    nc = bacc.Bacc("TRN2", target_bir_lowering=False, num_devices=1)
    arrays, args = {}, []
    for name in _INS:
        a = np.ascontiguousarray(inputs[name])
        arrays[f"in_{name}"] = a
        args.append(nc.dram_tensor(f"in_{name}", a.shape, mybir.dt.from_np(a.dtype), kind="ExternalInput").ap())
    args.append(nc.dram_tensor("out_0", (B, S, H), F32, kind="ExternalOutput").ap())
    build(nc, *args)
    r = run(nc, [arrays], core_ids=[0])
    return r.results[0]["out_0"]
```
